# Optimizing a Trainium2 kernel written in Bass

```python
import numpy as np
import jax
import jax.numpy as jnp

def _softmax(x, axis=-1):
    return jax.nn.softmax(x, axis=axis)

def _gelu(x):
    return jax.nn.gelu(x, approximate=True)

def _silu(x):
    return jax.nn.silu(x)

def _sigmoid(x):
    return jax.nn.sigmoid(x)

def _layernorm(x, axis=-1, eps=1e-05):
    m = jnp.mean(x, axis=axis, keepdims=True)
    v = jnp.var(x, axis=axis, keepdims=True)
    return (x - m) / jnp.sqrt(v + eps)

def _scatter_add(tgt, idx, src, axis=0):
    return tgt.at[idx].add(src)

def _segment_sum(src, seg, n):
    return jax.ops.segment_sum(src, seg, n)
kernel_name = 'mk_xattn_ffn_d1_seqx_r8_220e33'

def setup_inputs(seed: int=0):
    np.random.seed(seed)
    _w = jnp.asarray

    def _rec_inputs():
        import jax
        import jax.numpy as jnp
        _rk = jax.random.key(seed)
        x = 7.22e-05 + 1 * jax.random.normal(jax.random.fold_in(_rk, 1), (8, 256, 256), jnp.float32)
        _lenS = 256 - jax.random.randint(jax.random.fold_in(_rk, 7), (8,), 0, max(1, 256 // 4) + 1, jnp.int32)
        _lenS2 = 64 - jax.random.randint(jax.random.fold_in(_rk, 8), (8,), 0, max(1, 64 // 4) + 1, jnp.int32)
        _ctx_2048P = jax.random.normal(jax.random.fold_in(_rk, 11), (8, 16, 256), jnp.float32)
        _ctx_2048c = jax.random.dirichlet(jax.random.fold_in(_rk, 511), 0.3 * jnp.ones((16,), jnp.float32), (8, 64))
        _ctx_2048t = jnp.einsum('bsk,bkd->bsd', _ctx_2048c, _ctx_2048P)
        _ctx_2048t = _ctx_2048t * jax.lax.rsqrt(jnp.mean(jnp.square(_ctx_2048t)) + 1e-12) * 0.953939
        ctx_2048 = -0.000514642 + 1.00011 * (_ctx_2048t + 0.3 * jax.random.normal(jax.random.fold_in(_rk, 611), (8, 64, 256), jnp.float32))
        return (x, ctx_2048)
    x, ctx_2048 = _rec_inputs()

    def _L0_xattn_setup():
        import jax, jax.numpy as jnp
        import numpy as np
        D_MODEL = 256
        NUM_HEADS = 16
        HEAD_DIM = D_MODEL // NUM_HEADS

        def _fq_sym(x, axis):
            s = jnp.max(jnp.abs(x), axis=axis, keepdims=True) / 127.0
            s = jnp.maximum(s, 1e-08)
            q = jnp.clip(jnp.round(x / s), -127.0, 127.0) * s
            return x + jax.lax.stop_gradient(q - x)

        def _fq_unsigned(x, axis):
            s = jnp.max(x, axis=axis, keepdims=True) / 255.0
            s = jnp.maximum(s, 1e-08)
            q = jnp.clip(jnp.round(x / s), 0.0, 255.0) * s
            return x + jax.lax.stop_gradient(q - x)
        key = jax.random.key(seed)
        ks = jax.random.split(key, 8)
        B, N, M, C = (2, 256, 64, D_MODEL)
        return {'x': jax.random.normal(ks[0], (B, N, C), jnp.float32), 'cond': jax.random.normal(ks[1], (B, M, C), jnp.float32), 'Wq': jax.random.normal(ks[2], (C, C), jnp.float32) * 0.02, 'bq': jnp.zeros((C,), jnp.float32), 'Wkv': jax.random.normal(ks[3], (C, 2 * C), jnp.float32) * 0.02, 'bkv': jnp.zeros((2 * C,), jnp.float32), 'Wp': jax.random.normal(ks[4], (C, C), jnp.float32) * 0.02, 'bp': jnp.zeros((C,), jnp.float32)}
    _L0_xattn_all = _L0_xattn_setup()
    _L0_xattn_in = {k: v for k, v in _L0_xattn_all.items() if k in ('Wq', 'bq', 'Wkv', 'bkv', 'Wp', 'bp')}
    del _L0_xattn_all

    def _L0_ffn_setup():
        import jax, jax.numpy as jnp
        import numpy as np
        EPS = 1e-05

        def _weight_quant(w):
            s = 1.0 / jnp.clip(jnp.mean(jnp.abs(w)), EPS, None)
            return jnp.clip(jnp.round(w * s), -1.0, 1.0) / s

        def _act_quant(x):
            s = 127.0 / jnp.clip(jnp.max(jnp.abs(x), axis=-1, keepdims=True), EPS, None)
            return jnp.clip(jnp.round(x * s), -128.0, 127.0) / s

        def bitlinear(x, w):
            wq = w + jax.lax.stop_gradient(_weight_quant(w) - w)
            xq = x + jax.lax.stop_gradient(_act_quant(x) - x)
            return xq @ wq.T
        key = jax.random.key(seed)
        k = jax.random.split(key, 5)
        B, S, H, E, D = (4, 512, 256, 8, 256)
        x = jax.random.normal(k[0], (B, S, H), dtype=jnp.float32)
        router_w = jax.random.normal(k[1], (E, H), dtype=jnp.float32) * 0.02
        wg = jax.random.normal(k[2], (E, D, H), dtype=jnp.float32) * 0.02
        wu = jax.random.normal(k[3], (E, D, H), dtype=jnp.float32) * 0.02
        wd = jax.random.normal(k[4], (E, H, D), dtype=jnp.float32) * 0.02
        return {'x': x, 'router_w': router_w, 'wg': wg, 'wu': wu, 'wd': wd}
    _L0_ffn_all = _L0_ffn_setup()
    _L0_ffn_in = {k: v for k, v in _L0_ffn_all.items() if k in ('router_w', 'wg', 'wu', 'wd')}
    del _L0_ffn_all
    return {'x': x, 'ctx_2048': ctx_2048, 'L0_xattn_Wq': _L0_xattn_in['Wq'], 'L0_xattn_bq': _L0_xattn_in['bq'], 'L0_xattn_Wkv': _L0_xattn_in['Wkv'], 'L0_xattn_bkv': _L0_xattn_in['bkv'], 'L0_xattn_Wp': _L0_xattn_in['Wp'], 'L0_xattn_bp': _L0_xattn_in['bp'], 'L0_ffn_router_w': _L0_ffn_in['router_w'], 'L0_ffn_wg': _L0_ffn_in['wg'], 'L0_ffn_wu': _L0_ffn_in['wu'], 'L0_ffn_wd': _L0_ffn_in['wd']}

def reference(x, ctx_2048, L0_xattn_Wq, L0_xattn_bq, L0_xattn_Wkv, L0_xattn_bkv, L0_xattn_Wp, L0_xattn_bp, L0_ffn_router_w, L0_ffn_wg, L0_ffn_wu, L0_ffn_wd):
    import jax
    import jax.numpy as jnp

    def _L0_xattn_ref(x, cond, Wq, bq, Wkv, bkv, Wp, bp):
        import jax, jax.numpy as jnp
        import numpy as np
        D_MODEL = 256
        NUM_HEADS = 16
        HEAD_DIM = D_MODEL // NUM_HEADS

        def _fq_sym(x, axis):
            s = jnp.max(jnp.abs(x), axis=axis, keepdims=True) / 127.0
            s = jnp.maximum(s, 1e-08)
            q = jnp.clip(jnp.round(x / s), -127.0, 127.0) * s
            return x + jax.lax.stop_gradient(q - x)

        def _fq_unsigned(x, axis):
            s = jnp.max(x, axis=axis, keepdims=True) / 255.0
            s = jnp.maximum(s, 1e-08)
            q = jnp.clip(jnp.round(x / s), 0.0, 255.0) * s
            return x + jax.lax.stop_gradient(q - x)
        B, N, C = x.shape
        H, hd = (NUM_HEADS, HEAD_DIM)
        q = (x @ Wq + bq).reshape(1, B * N, H, hd)
        kv = (cond @ Wkv + bkv).reshape(1, -1, 2, H, hd)
        k, v = (kv[:, :, 0], kv[:, :, 1])
        scale = 1.0 / np.sqrt(hd).astype(np.float32)
        q = jnp.transpose(q * scale, (0, 2, 1, 3))
        k = jnp.transpose(k, (0, 2, 1, 3))
        v = jnp.transpose(v, (0, 2, 1, 3))
        q = _fq_sym(q, axis=-1)
        k = _fq_sym(k, axis=-1)
        v = _fq_sym(v, axis=2)
        attn = jnp.einsum('bhqd,bhkd->bhqk', q, k)
        attn = jax.nn.softmax(attn.astype(jnp.float32), axis=-1)
        attn = _fq_unsigned(attn, axis=-1)
        out = jnp.einsum('bhqk,bhkd->bhqd', attn, v)
        out = jnp.transpose(out, (0, 2, 1, 3)).reshape(B, N, C)
        return out @ Wp + bp

    def _L0_ffn_ref(x, router_w, wg, wu, wd):
        import jax, jax.numpy as jnp
        import numpy as np
        EPS = 1e-05

        def _weight_quant(w):
            s = 1.0 / jnp.clip(jnp.mean(jnp.abs(w)), EPS, None)
            return jnp.clip(jnp.round(w * s), -1.0, 1.0) / s

        def _act_quant(x):
            s = 127.0 / jnp.clip(jnp.max(jnp.abs(x), axis=-1, keepdims=True), EPS, None)
            return jnp.clip(jnp.round(x * s), -128.0, 127.0) / s

        def bitlinear(x, w):
            wq = w + jax.lax.stop_gradient(_weight_quant(w) - w)
            xq = x + jax.lax.stop_gradient(_act_quant(x) - x)
            return xq @ wq.T
        B, S, H = x.shape
        E = wg.shape[0]
        logits = jnp.einsum('bsh,eh->bse', x, router_w)
        idx = jnp.argmax(logits, axis=-1).reshape(-1)
        xf = x.reshape(-1, H)
        out = jnp.zeros_like(xf)
        for e in range(E):
            g = bitlinear(xf, wg[e])
            u = bitlinear(xf, wu[e])
            y = bitlinear(jnp.square(jax.nn.relu(g)) * u, wd[e])
            out = out + jnp.where((idx == e)[:, None], y, 0.0)
        return out.reshape(B, S, H)
    x = x + _L0_xattn_ref(_layernorm(x, axis=-1), ctx_2048, L0_xattn_Wq, L0_xattn_bq, L0_xattn_Wkv, L0_xattn_bkv, L0_xattn_Wp, L0_xattn_bp)
    x = x + _L0_ffn_ref(_layernorm(x, axis=-1), L0_ffn_router_w, L0_ffn_wg, L0_ffn_wu, L0_ffn_wd)
    return x

_drawn_inputs = setup_inputs


def setup_inputs(seed=0):
    import zlib

    import numpy as np

    out = dict(_drawn_inputs(seed))
    spreads = {'L0_xattn_bq': (0.0, 0.8), 'L0_xattn_bkv': (0.0, 0.1), 'L0_xattn_bp': (0.0, 0.1)}
    factors = {'ctx_2048': 3.045,
     'L0_xattn_Wq': 8.0,
     'L0_xattn_Wkv': 3.498,
     'L0_ffn_router_w': 8.0,
     'L0_ffn_wg': 8.0,
     'L0_ffn_wu': 8.0,
     'L0_ffn_wd': 8.0}
    for name, (base, spread) in spreads.items():
        noise = np.random.default_rng([zlib.crc32(name.encode()), seed]).standard_normal(out[name].shape)
        drawn = base * np.exp(spread * noise) if base else spread * noise
        out[name] = jnp.asarray(drawn.astype(out[name].dtype))
    for name, factor in factors.items():
        out[name] = (out[name] * factor).astype(out[name].dtype)
    return out
```

```python
import concourse.bass as bass
from concourse import mybir
from contextlib import ExitStack
import math


class Signal:

    def __init__(self, sem, per_tile):
        self.sem, self.per_tile = sem, per_tile

    def value(self, tile, nth):
        register, offset = tile
        fixed = self.per_tile * offset + nth
        return fixed if register is None else register * self.per_tile + fixed


def cross_attention_moe(nc, x, ctx_t, wq, bq, wkv, bk, bv, wp, bp, router, w_gate_up, w_down, out):
    fp32, bf16, fp16 = mybir.dt.float32, mybir.dt.bfloat16, mybir.dt.float16
    u8, u16, i32 = mybir.dt.uint8, mybir.dt.uint16, mybir.dt.int32
    ALU = mybir.AluOpType
    ACT = mybir.ActivationFunctionType
    AX = mybir.AxisListType

    P = 128
    TOKENS, D = x.shape
    KEYS = ctx_t.shape[1]
    EXPERTS = router.shape[2]
    HEADS = 16
    HD = D // HEADS
    DC = D // P
    KC = KEYS // P
    TILES = TOKENS // P
    PAIRS = HEADS // 2
    PARTS = 3
    SLOT = 64
    ROWS = PARTS * HD
    G = HEADS * TILES // 2
    MAGIC = 1.5 * 2.0 ** 23
    LEVELS = 255.0
    OFFSET = 1024.0
    LN_EPS = 1e-5
    Q_EPS = 1e-5
    S_EPS = 1e-8

    x_v = x.rearrange("(t p) c -> t p c", p=P)
    out_v = out.rearrange("(t p) c -> t p c", p=P)

    ctx = ExitStack()
    with ctx:
        def sb(name, shape, dt):
            return ctx.enter_context(nc.sbuf_tensor(name, shape, dt))

        def pb(name, shape, dt):
            return ctx.enter_context(nc.psum_tensor(name, shape, dt))

        def sem(name):
            return ctx.enter_context(nc.semaphore(name))

        def signal(name, per_tile=1):
            return Signal(sem(name), per_tile)

        ctxT = sb("ctxT", [P, DC, KEYS], fp32)
        wq_sb = sb("wq_sb", [P, DC, D], fp32)
        wkv_sb = sb("wkv_sb", [P, DC, 2 * D], fp32)
        wp_raw = sb("wp_raw", [P, DC, D], fp32)
        wp_sb = sb("wp_sb", [P, DC, D], fp32)
        bq_sb = sb("bq_sb", [P, D], fp32)
        bk_sb = sb("bk_sb", [P, D], fp32)
        bv_sb = sb("bv_sb", [P, DC], fp32)
        bp_sb = sb("bp_sb", [P, D], fp32)
        rT = sb("rT", [P, DC, EXPERTS], fp32)
        gu_raw = sb("gu_raw", [P, DC, EXPERTS, 2, D], fp32)
        dn_raw = sb("dn_raw", [P, DC, EXPERTS, D], fp32)
        gu_w = sb("gu_w", [P, DC, EXPERTS, 2, D], bf16)
        dn_w = sb("dn_w", [P, DC, EXPERTS, D], bf16)
        w_abs = sb("w_abs", [P, 3, EXPERTS], fp32)
        w_scratch = sb("w_scratch", [P, DC, D], bf16)
        w_step = sb("w_step", [P, 3, EXPERTS], fp32)
        w_inv = sb("w_inv", [P, 3, EXPERTS], fp32)
        tab = sb("tab", [P, 2, EXPERTS], fp32)
        tab_t = sb("tab_t", [P, EXPERTS], fp32)
        ident = sb("ident", [P, P], fp32)
        ident_b = sb("ident_b", [P, P], bf16)
        ident_h = sb("ident_h", [P, P], fp16)
        ones = sb("ones", [P, P], fp32)
        minus_off = sb("minus_off", [P, P], fp16)
        minus_half = sb("minus_half", [P, 1], fp32)
        eps = sb("eps", [P, 1], fp32)
        ln_levels = sb("ln_levels", [P, 2], fp32)
        head_scale = sb("head_scale", [P, 2, HEADS], fp32)
        order = sb("order", [P, EXPERTS], fp32)
        kT = sb("kT", [P, PAIRS, KEYS], bf16)
        V = sb("V", [P, KC, D], fp16)

        kb = sb("kb", [P, D], fp32)
        k_max = sb("k_max", [P, HEADS], fp32)
        k_step = sb("k_step", [P, HEADS], fp32)
        k_inv = sb("k_inv", [P, HEADS], fp32)
        k_s = sb("k_s", [P, D], fp32)
        k_i = sb("k_i", [P, D], fp32)
        k_q = sb("k_q", [P, D], fp32)
        k_r1 = sb("k_r1", [P, D], fp32)
        k_r2 = sb("k_r2", [P, D], fp32)
        k_rep = sb("k_rep", [P, HEADS, SLOT], bf16)
        vb = sb("vb", [P, DC, KEYS], fp32)
        v_max = sb("v_max", [P, DC], fp32)
        v_step = sb("v_step", [P, DC], fp32)
        v_inv = sb("v_inv", [P, DC], fp32)
        v_s = sb("v_s", [P, DC, KEYS], fp32)
        v_i = sb("v_i", [P, DC, KEYS], fp16)

        x_ln = sb("x_ln", [P, 2, D], fp32)
        x_res = sb("x_res", [P, 2, D], fp32)
        bn1 = sb("bn1", [P, 6], fp32)
        mv1 = sb("mv1", [P, 2], fp32)
        var1 = sb("var1", [P, 1], fp32)
        rstd1 = sb("rstd1", [P, 1], fp32)
        ln1 = sb("ln1", [P, D], fp32)
        lnT1 = sb("lnT1", [P, DC, P], fp32)
        qb = sb("qb", [P, D], fp32)
        q_max = sb("q_max", [P, HEADS], fp32)
        q_step = sb("q_step", [P, HEADS], fp32)
        q_inv = sb("q_inv", [P, HEADS], fp32)
        q_s = sb("q_s", [P, D], fp32)
        q_rep = sb("q_rep", [P, HEADS, SLOT], bf16)
        q_scale = sb("q_scale", [P, 2, HEADS], fp32)
        q_nscale = sb("q_nscale", [P, 2, HEADS], fp32)
        qT = sb("qT", [P, 2, PAIRS, P], bf16)
        s_max = sb("s_max", [P, 2, 2], fp32)
        nb0 = sb("nb0", [P, 2, 2], fp32)
        nb = sb("nb", [P, 2, 2], fp32)
        probs = sb("probs", [P, 2, 2, KEYS], fp16)
        probsT = sb("probsT", [P, 2, 2 * KC, P], fp16)
        z = sb("z", [P, 2, HEADS], fp32)
        rz = sb("rz", [P, HEADS], fp32)
        attn = sb("attn", [P, D], fp32)
        attnT = sb("attnT", [P, DC, P], fp32)
        xb = sb("xb", [P, D], fp32)
        x2 = sb("x2", [P, 2, D], fp32)
        bn2 = sb("bn2", [P, 6], fp32)
        mv2 = sb("mv2", [P, 2], fp32)
        var2 = sb("var2", [P, 1], fp32)
        rstd2 = sb("rstd2", [P, 1], fp32)
        ln2 = sb("ln2", [P, D], fp32)
        lnT2 = sb("lnT2", [P, DC, P], fp32)
        a_max = sb("a_max", [P, 1], fp32)
        a_step = sb("a_step", [P, 1], fp32)
        a_inv = sb("a_inv", [P, 1], fp32)
        a_m = sb("a_m", [P, D], fp32)
        a_q = sb("a_q", [P, D], bf16)
        aT = sb("aT", [P, DC, P], bf16)
        l_max = sb("l_max", [P, 1], fp32)
        l_rank = sb("l_rank", [P, EXPERTS], fp32)
        l_top = sb("l_top", [P, 1], fp32)
        mask = sb("mask", [P, EXPERTS], bf16)
        sel_t = sb("sel_t", [P, 2, EXPERTS], fp32)
        sel = sb("sel", [P, 2, 2], fp32)
        c1 = sb("c1", [P, 1], fp32)
        c2 = sb("c2", [P, 1], fp32)
        h_scale = sb("h_scale", [P, 2, 1], fp32)
        maskT = sb("maskT", [P, EXPERTS, P], bf16)
        am = sb("am", [P, DC, EXPERTS, P], bf16)
        g_relu = sb("g_relu", [P, D], fp32)
        gu = sb("gu", [P, D], fp32)
        h = sb("h", [P, D], fp32)
        h_max = sb("h_max", [P, 1], fp32)
        h_abs = sb("h_abs", [P, 1], fp32)
        h_inv = sb("h_inv", [P, 1], fp32)
        h_mul = sb("h_mul", [P, 1], fp32)
        y_scale = sb("y_scale", [P, 1], fp32)
        h_m = sb("h_m", [P, D], fp32)
        h_q = sb("h_q", [P, D], bf16)
        hT = sb("hT", [P, DC, P], bf16)
        hm = sb("hm", [P, DC, EXPERTS, P], bf16)
        y = sb("y", [P, 2, D], fp32)

        scores = [pb(f"scores{i}", [P, 2, KEYS], fp32) for i in range(2)]
        turned = pb("turned", [P, 2 * KC, P], fp16)
        heads_out = pb("heads_out", [P, 2 * D], fp32)
        front = pb("front", [P, 2 * D], fp32)
        ffn = pb("ffn", [P, 2 * D], fp32)
        front_b = front[:, :].bitcast(bf16).rearrange("p (n q) -> p n q", q=P)
        ffn_b = ffn[:, :].bitcast(bf16).rearrange("p (n q) -> p n q", q=P)

        got_kv = sem("got_kv")
        got_front = sem("got_front")
        got_proj = sem("got_proj")
        got_router = sem("got_router")
        got_experts = [sem(f"got_experts{e}") for e in range(EXPERTS)]
        zero_ready = sem("zero_ready")
        consts_ready = sem("consts_ready")
        idents_ready = sem("idents_ready")
        k_psum = sem("k_psum")
        k_read = sem("k_read")
        k_chain = sem("k_chain")
        k_rep_ready = sem("k_rep_ready")
        kT_psum = sem("kT_psum")
        kT_ready = sem("kT_ready")
        v_psum = sem("v_psum")
        v_read = sem("v_read")
        v_chain = sem("v_chain")
        v_int_ready = sem("v_int_ready")
        V_psum = sem("V_psum")
        V_ready = sem("V_ready")
        wp_ready = sem("wp_ready")
        w_abs_ready = sem("w_abs_ready")
        w_sum_psum = sem("w_sum_psum")
        w_step_ready = sem("w_step_ready")
        w_chain = sem("w_chain")
        w_scaled = sem("w_scaled")
        w_clipped = sem("w_clipped")
        w_ready = sem("w_ready")

        x_ln_in = [sem(f"x_ln_in{i}") for i in range(2)]
        x_res_in = [sem(f"x_res_in{i}") for i in range(2)]
        y_out = [sem(f"y_out{i}") for i in range(2)]
        bn1_done = signal("bn1_done")
        mv1_done = signal("mv1_done")
        var1_done = signal("var1_done")
        rstd1_done = signal("rstd1_done")
        ln1_done = signal("ln1_done")
        lnT1_psum = signal("lnT1_psum")
        lnT1_done = signal("lnT1_done")
        q_psum = signal("q_psum")
        qb_done = signal("qb_done")
        q_chain = signal("q_chain", 4)
        q_scale_done = signal("q_scale_done", 2)
        q_rep_done = signal("q_rep_done")
        qT_psum = signal("qT_psum")
        qT_done = signal("qT_done")
        scores_done = signal("scores_done", PAIRS)
        max_done = signal("max_done", PAIRS)
        nb0_done = signal("nb0_done", PAIRS)
        nb_done = signal("nb_done", PAIRS)
        exp_done = signal("exp_done", HEADS)
        turned_done = signal("turned_done", PAIRS)
        probsT_done = signal("probsT_done", PAIRS)
        pv_done = signal("pv_done", PAIRS)
        rz_done = signal("rz_done")
        attn_done = signal("attn_done")
        attnT_psum = signal("attnT_psum")
        attnT_done = signal("attnT_done")
        proj_psum = signal("proj_psum")
        xb_done = signal("xb_done")
        x2_done = signal("x2_done")
        bn2_done = signal("bn2_done")
        mv2_done = signal("mv2_done")
        var2_done = signal("var2_done")
        rstd2_done = signal("rstd2_done")
        ln2_done = signal("ln2_done")
        lnT2_psum = signal("lnT2_psum")
        lnT2_done = signal("lnT2_done")
        logits_psum = signal("logits_psum")
        a_chain = signal("a_chain", 4)
        a_q_done = signal("a_q_done")
        l_chain = signal("l_chain", 3)
        mask_done = signal("mask_done")
        sel_chain = signal("sel_chain")
        sel_done = signal("sel_done")
        c_chain = signal("c_chain", 2)
        h_scale_done = signal("h_scale_done")
        aT_psum = signal("aT_psum")
        aT_done = signal("aT_done")
        maskT_psum = signal("maskT_psum")
        maskT_done = signal("maskT_done")
        am_done = signal("am_done", DC)
        gu_psum = signal("gu_psum")
        relu_done = signal("relu_done")
        gu_done = signal("gu_done")
        h_done = signal("h_done")
        h_chain = signal("h_chain", 4)
        y_scale_done = signal("y_scale_done")
        h_m_done = signal("h_m_done")
        h_q_done = signal("h_q_done")
        hT_psum = signal("hT_psum")
        hT_done = signal("hT_done")
        hm_done = signal("hm_done", DC)
        y_psum = signal("y_psum")
        y_done = signal("y_done")

        def shift(tile, by):
            return tile[0], tile[1] + by

        def number(tile):
            return tile[1] if tile[0] is None else None

        def exists(tile):
            return tile[0] is not None or 0 <= tile[1] < TILES

        def unit(tile, pair):
            return shift(tile, pair // PAIRS), pair % PAIRS

        def after(eng, what, tile, nth=None):
            if not exists(tile):
                return
            eng.wait_ge(what.sem, what.value(tile, what.per_tile if nth is None else nth))

        def parity(tile):
            return tile[1] % 2

        LOOP_FROM, LOOP_TO = 4, TILES - 2
        ENDS = TILES + 3

        def run(eng, body):
            for t in range(LOOP_FROM):
                body((None, t))
            with eng.Fori(0, (LOOP_TO - LOOP_FROM) // 2) as turn:
                body((turn * 2, LOOP_FROM))
                body((turn * 2, LOOP_FROM + 1))
            for t in range(LOOP_TO, ENDS):
                body((None, t))

        block = ctx.enter_context(nc.Block())

        @block.sync
        def _(sp):
            sp.dma_start(ctxT[:, :, :], ctx_t.rearrange("(c p) k -> p c k", p=P)).then_inc(got_kv, 16)
            sp.dma_start(wkv_sb[:, :, :], wkv.rearrange("(c p) n -> p c n", p=P)).then_inc(got_kv, 16)
            sp.dma_start(bk_sb[:, :], bk.broadcast_to([P, D])).then_inc(got_kv, 16)
            sp.dma_start(bv_sb[:, :], bv).then_inc(got_kv, 16)
            for t in range(2):
                sp.dma_start(x_ln[:, t, :], x_v[t]).then_inc(x_ln_in[t], 16)
            sp.dma_start(wq_sb[:, :, :], wq.rearrange("(c p) n -> p c n", p=P)).then_inc(got_front, 16)
            sp.dma_start(bq_sb[:, :], bq.broadcast_to([P, D])).then_inc(got_front, 16)
            sp.dma_start(wp_raw[:, :, :], wp.rearrange("(c p) n -> p c n", p=P)).then_inc(got_proj, 16)
            sp.dma_start(bp_sb[:, :], bp.broadcast_to([P, D])).then_inc(got_proj, 16)
            sp.dma_start(rT[:, :, :], router.rearrange("c p e -> p c e")).then_inc(got_router, 16)
            for t in range(2):
                sp.dma_start(x_res[:, t, :], x_v[t]).then_inc(x_res_in[t], 16)

            def tile_io(t):
                if exists(shift(t, 2)):
                    after(sp, ln1_done, t)
                    load(x_ln, x_ln_in, shift(t, 2))
                if exists(shift(t, 1)) and number(t) != 0:
                    after(sp, xb_done, shift(t, -1))
                    load(x_res, x_res_in, shift(t, 1))
                if exists(shift(t, -3)):
                    s = shift(t, -3)
                    after(sp, y_done, s)
                    sp.dma_start(rows(out_v, s), y[:, parity(s), :]).then_inc(y_out[parity(s)], 16)

            def rows(v, t):
                return v[t[1]] if t[0] is None else v[t[0] + t[1]]

            def load(into, arrived, t):
                sp.dma_start(into[:, parity(t), :], rows(x_v, t)).then_inc(arrived[parity(t)], 16)

            run(sp, tile_io)
            for i in range(2):
                sp.wait_ge(y_out[i], 16 * (TILES // 2 + 1))

        def arrived(eng, sems, t):
            p = parity(t)
            if t[0] is None:
                eng.wait_ge(sems[p], 16 * (t[1] // 2 + 1))
            else:
                eng.wait_ge(sems[p], t[0] * 8 + (8 * (t[1] - p) + 16))

        @block.scalar
        def _(act):
            for e in range(EXPERTS):
                act.dma_start(gu_raw[:, :, e, :, :], w_gate_up[:, :, e].rearrange("c p a n -> p c a n")) \
                    .then_inc(got_experts[e], 16)
                act.dma_start(dn_raw[:, :, e, :], w_down[:, :, e].rearrange("c p n -> p c n")) \
                    .then_inc(got_experts[e], 16)
            n = 0
            for e in range(EXPERTS):
                act.wait_ge(got_experts[e], 32)
                for m in range(3):
                    w = gu_raw[:, :, e, m, :] if m < 2 else dn_raw[:, :, e, :]
                    if n:
                        act.wait_ge(w_abs_ready, n)
                    nc.scalar.activation(w_scratch[:, :, :], w, ACT.Abs,
                                         accum_out=w_abs[:, m, e:e + 1]).then_inc(w_abs_ready, 1)
                    n += 1

            def lnT1_copy(t):
                after(act, lnT1_psum, t)
                after(act, hT_psum, shift(t, -4))
                nc.scalar.activation(lnT1[:, :, :], front[:, 0:D].rearrange("p (c q) -> p c q", q=P),
                                     ACT.Copy).then_inc(lnT1_done.sem, 1)

            def exps(t, pair):
                t, pair = unit(t, pair)
                if not exists(t):
                    return
                after(act, nb_done, t, pair + 1)
                before, b_pair = unit(t, pair - 2)
                after(act, turned_done, before, b_pair + 1)
                i = pair % 2
                low = probs[:, i, :, :].rearrange("p a b -> p (a b)").bitcast(u8) \
                    .rearrange("p (a b two) -> p a b two", a=2, two=2)
                for j in range(2):
                    hd = 2 * pair + j
                    if j == 0 and pair == 0:
                        after(act, rz_done, shift(t, -2))
                    nc.scalar.activation(low[:, j, :, 0], scores[i][:, j, :], ACT.Exp,
                                         bias=nb[:, i, j:j + 1], scale=q_scale[:, parity(t), hd:hd + 1],
                                         accum_out=z[:, parity(t), hd:hd + 1]).then_inc(exp_done.sem, 1)

            def probsT_copy(t, pair):
                after(act, turned_done, t, pair + 1)
                before, b_pair = unit(t, pair - 2)
                after(act, pv_done, before, b_pair + 1)
                nc.scalar.activation(probsT[:, pair % 2, :, :].bitcast(fp32), turned[:, :, :].bitcast(fp32),
                                     ACT.Copy).then_inc(probsT_done.sem, 1)

            lnT1_copy((None, 0))
            act.wait_ge(consts_ready, 1)
            exps((None, 0), 0)

            def tile_work(t):
                for u in range(PAIRS):
                    exps(t, u + 1)
                    if exists(t):
                        probsT_copy(t, u)
                    if u == 0 and exists(shift(t, 1)):
                        lnT1_copy(shift(t, 1))
                    if u == 0 and exists(shift(t, -3)):
                        after(act, hT_psum, shift(t, -3))
                        nc.scalar.activation(hT[:, :, :], front_b[:, 2 * DC:3 * DC, :], ACT.Copy) \
                            .then_inc(hT_done.sem, 1)
                    if u == 2 and exists(shift(t, -1)):
                        after(act, attnT_psum, shift(t, -1))
                        nc.scalar.activation(attnT[:, :, :], front[:, 0:D].rearrange("p (c q) -> p c q", q=P),
                                             ACT.Copy).then_inc(attnT_done.sem, 1)
                    if u == 5 and exists(shift(t, -1)):
                        after(act, lnT2_psum, shift(t, -1))
                        nc.scalar.activation(lnT2[:, :, :], front[:, 0:D].rearrange("p (c q) -> p c q", q=P),
                                             ACT.Copy).then_inc(lnT2_done.sem, 1)
                    if u == 6 and exists(shift(t, -2)):
                        after(act, gu_psum, shift(t, -2))
                        nc.scalar.activation(g_relu[:, :], ffn[:, 0:D], ACT.Relu).then_inc(relu_done.sem, 1)

            run(act, tile_work)

        @block.gpsimd
        def _(pool):
            pool.wait_ge(zero_ready, 1)
            nc.gpsimd.affine_select(out=ident[:, :], in_=ident[:, :], compare_op=ALU.not_equal, fill=1.0,
                                    base=0, pattern=[[-1, P]], channel_multiplier=1).then_inc(idents_ready, 1)

            def rstd(t, mv, mv_done, var, v_done, r, done):
                after(pool, mv_done, t)
                nc.gpsimd.tensor_tensor(var[:, :], mv[:, 1:2], eps[:, :], ALU.add) \
                    .then_inc(v_done.sem, 1)
                after(pool, v_done, t)
                nc.gpsimd.tensor_tensor(r[:, :], var[:, :], minus_half[:, :], ALU.pow).then_inc(done.sem, 1)

            def bias(t, pair):
                t, pair = unit(t, pair)
                if not exists(t):
                    return
                i = pair % 2
                after(pool, max_done, t, pair + 1)
                if pair == 0:
                    after(pool, q_scale_done, t)
                before, b_pair = unit(t, pair - 2)
                after(pool, exp_done, before, 2 * b_pair + 2)
                nc.gpsimd.tensor_tensor(nb0[:, i, :], s_max[:, i, :],
                                        q_nscale[:, parity(t), 2 * pair:2 * pair + 2], ALU.mult) \
                    .then_inc(nb0_done.sem, 1)
                after(pool, nb0_done, t, pair + 1)
                nc.gpsimd.tensor_tensor(nb[:, i, :], nb0[:, i, :], ln_levels[:, :], ALU.add) \
                    .then_inc(nb_done.sem, 1)

            def q_scales(t):
                after(pool, q_chain, t, 2)
                before = shift(t, -2)
                after(pool, exp_done, before)
                for i, scaled in enumerate((q_nscale, q_scale)):
                    nc.gpsimd.tensor_tensor(scaled[:, parity(t), :], q_step[:, :], head_scale[:, i, :],
                                            ALU.mult).then_inc(q_scale_done.sem, 1)

            rstd((None, 0), mv1, mv1_done, var1, var1_done, rstd1, rstd1_done)
            rstd((None, 1), mv1, mv1_done, var1, var1_done, rstd1, rstd1_done)
            q_scales((None, 0))
            bias((None, 0), 0)
            bias((None, 0), 1)

            def weights_scaled(n):
                m, e = n % 3, n // 3
                w = gu_raw[:, :, e, m, :] if m < 2 else dn_raw[:, :, e, :]
                pool.wait_ge(w_step_ready, 2)
                nc.gpsimd.tensor_scalar(w, w, w_inv[:, m, e:e + 1], MAGIC, ALU.mult, ALU.add) \
                    .then_inc(w_scaled, 1)

            def tile_work(t):
                for u in range(PAIRS):
                    bias(t, u + 2)
                    if t[0] is None and t[1] < 2 and 8 * t[1] + u < 12:
                        weights_scaled(2 * (8 * t[1] + u))
                        weights_scaled(2 * (8 * t[1] + u) + 1)
                    if u == 2 and exists(shift(t, 1)):
                        q_scales(shift(t, 1))
                    if u == 4 and exists(shift(t, -1)):
                        rstd(shift(t, -1), mv2, mv2_done, var2, var2_done, rstd2, rstd2_done)
                    if u == 5 and exists(shift(t, -1)):
                        s = shift(t, -1)
                        after(pool, a_chain, s, 4)
                        nc.gpsimd.tensor_tensor(c1[:, :], a_step[:, :], a_step[:, :], ALU.mult) \
                            .then_inc(c_chain.sem, 1)
                        nc.gpsimd.tensor_scalar(a_q[:, :], a_m[:, :], -MAGIC, 1.0, ALU.add, ALU.mult) \
                            .then_inc(a_q_done.sem, 1)
                    if u == 7 and exists(shift(t, -1)):
                        s = shift(t, -1)
                        after(pool, sel_done, s)
                        nc.gpsimd.tensor_tensor(c2[:, :], a_step[:, :], sel[:, parity(s), 0:1], ALU.mult) \
                            .then_inc(c_chain.sem, 1)
                        after(pool, c_chain, s)
                        nc.gpsimd.tensor_tensor(h_scale[:, parity(s), :], c1[:, :], c2[:, :], ALU.mult) \
                            .then_inc(h_scale_done.sem, 1)
                    if u == 7 and exists(shift(t, -2)):
                        s = shift(t, -2)
                        after(pool, h_m_done, s)
                        after(pool, y_done, shift(s, -1))
                        nc.gpsimd.tensor_tensor(y_scale[:, :], h_abs[:, :], sel[:, parity(s), 1:2], ALU.mult) \
                            .then_inc(y_scale_done.sem, 1)
                        nc.gpsimd.tensor_scalar(h_q[:, :], h_m[:, :], -MAGIC, 1.0, ALU.add, ALU.mult) \
                            .then_inc(h_q_done.sem, 1)
                    if u == 7 and exists(shift(t, 2)):
                        rstd(shift(t, 2), mv1, mv1_done, var1, var1_done, rstd1, rstd1_done)

            run(pool, tile_work)

        @block.vector
        def _(dve):
            nc.vector.memset(ident[:, :], 0.0)
            nc.vector.memset(minus_half[:, :], -0.5)
            nc.vector.memset(eps[:, :], LN_EPS)
            nc.vector.memset(ln_levels[:, :], math.log(LEVELS))
            nc.vector.memset(head_scale[:, 0, :], -1.0 / math.sqrt(HD))
            nc.vector.memset(head_scale[:, 1, :], 1.0 / math.sqrt(HD)).then_inc(zero_ready, 1)
            nc.vector.memset(ones[:, :], 1.0)
            nc.vector.memset(minus_off[:, :], -OFFSET)
            nc.vector.memset(k_rep[:, :, :], 0.0)
            nc.vector.memset(q_rep[:, :, :], 0.0)
            for e in range(EXPERTS):
                nc.vector.memset(order[:, e:e + 1], float(EXPERTS - e))
            for i in range(2):
                nc.vector.memset(y[:, i, :], 0.0).then_inc(y_out[i], 16)
            nc.vector.memset(probs[:, :, :, :], OFFSET).then_inc(consts_ready, 1)
            dve.wait_ge(idents_ready, 1)
            nc.vector.tensor_copy(ident_b[:, :], ident[:, :]).then_inc(idents_ready, 1)
            nc.vector.tensor_copy(ident_h[:, :], ident[:, :]).then_inc(idents_ready, 1)

            def first_stats(t):
                arrived(dve, x_ln_in, t)
                nc.vector.bn_stats(bn1[:, :], x_ln[:, parity(t), :]).then_inc(bn1_done.sem, 1)

            def first_norm(t):
                nc.vector.bn_aggr(mv1[:, :], bn1[:, :]).then_inc(mv1_done.sem, 1)
                after(dve, rstd1_done, t)
                after(dve, lnT1_psum, shift(t, -1))
                nc.vector.tensor_scalar(ln1[:, :], x_ln[:, parity(t), :], mv1[:, 0:1], rstd1[:, :],
                                        ALU.subtract, ALU.mult).then_inc(ln1_done.sem, 1)

            def queries(t):
                after(dve, q_psum, t)
                nc.vector.tensor_tensor(qb[:, :], front[:, 0:D], bq_sb[:, :], ALU.add).then_inc(qb_done.sem, 1)
                after(dve, qb_done, t)
                nc.vector.tensor_reduce(q_max[:, :], qb[:, :].rearrange("p (h d) -> p h d", d=HD), axis=AX.X,
                                        op=ALU.max, apply_absolute_value=True).then_inc(q_chain.sem, 1)
                after(dve, q_chain, t, 1)
                after(dve, q_scale_done, shift(t, -1))
                nc.vector.tensor_scalar(q_step[:, :], q_max[:, :], 1.0 / 127.0, S_EPS * math.sqrt(HD),
                                        ALU.mult, ALU.max).then_inc(q_chain.sem, 1)
                after(dve, q_chain, t, 2)
                nc.vector.reciprocal(q_inv[:, :], q_step[:, :]).then_inc(q_chain.sem, 1)
                after(dve, q_chain, t, 3)
                nc.vector.tensor_tensor(q_s[:, :].rearrange("p (h d) -> p h d", d=HD),
                                        qb[:, :].rearrange("p (h d) -> p h d", d=HD),
                                        q_inv[:, :].unsqueeze(2).broadcast_to([P, HEADS, HD]),
                                        ALU.mult).then_inc(q_chain.sem, 1)

            def query_parts(t):
                after(dve, q_chain, t, 4)
                after(dve, qT_psum, shift(t, -1))
                nc.vector.tensor_scalar(
                    q_rep[:, :, 0:ROWS].rearrange("p h (r d) -> p h r d", d=HD),
                    q_s[:, :].rearrange("p (h d) -> p h d", d=HD).unsqueeze(2).broadcast_to([P, HEADS, PARTS, HD]),
                    MAGIC, MAGIC, ALU.add, ALU.subtract).then_inc(q_rep_done.sem, 1)

            def qT_copy(t):
                after(dve, qT_psum, t)
                after(dve, scores_done, shift(t, -2))
                nc.vector.tensor_copy(qT[:, parity(t), :, :].bitcast(i32), front_b.bitcast(i32)) \
                    .then_inc(qT_done.sem, 1)

            def maxima(t, pair):
                t, pair = unit(t, pair)
                if not exists(t):
                    return
                after(dve, scores_done, t, pair + 1)
                nc.vector.tensor_reduce(s_max[:, pair % 2, :], scores[pair % 2][:, :, :], axis=AX.X, op=ALU.max) \
                    .then_inc(max_done.sem, 1)

            dve.wait_ge(got_kv, 64)
            n = 0

            def link(ins):
                nonlocal n
                n += 1
                ins.then_inc(k_chain, 1)
                dve.wait_ge(k_chain, n)

            def by_head(a):
                return a[:, :].rearrange("p (h d) -> p h d", d=HD)

            def spread(a):
                return a[:, :].unsqueeze(2).broadcast_to([P, HEADS, HD])

            def part(j):
                return k_rep[:, :, j * HD:(j + 1) * HD]

            for k in range(KC):
                dve.wait_ge(k_psum, k + 1)
                bank = ffn if k % 2 == 0 else heads_out
                nc.vector.tensor_tensor(kb[:, :], bank[:, 0:D], bk_sb[:, :], ALU.add).then_inc(k_read, 1)
                dve.wait_ge(k_read, k + 1)
                link(nc.vector.tensor_reduce(k_max[:, :], by_head(kb), axis=AX.X, op=ALU.max,
                                             apply_absolute_value=True))
                link(nc.vector.tensor_scalar(k_step[:, :], k_max[:, :], 1.0 / 127.0, S_EPS, ALU.mult, ALU.max))
                link(nc.vector.reciprocal(k_inv[:, :], k_step[:, :]))
                link(nc.vector.tensor_tensor(by_head(k_s), by_head(kb), spread(k_inv), ALU.mult))
                link(nc.vector.tensor_scalar(k_i[:, :], k_s[:, :], MAGIC, MAGIC, ALU.add, ALU.subtract))
                link(nc.vector.tensor_tensor(by_head(k_q), by_head(k_i), spread(k_step), ALU.mult))
                if k:
                    dve.wait_ge(kT_psum, k)
                link(nc.vector.tensor_copy(part(0), by_head(k_q)))
                link(nc.vector.tensor_tensor(by_head(k_r1), by_head(k_q), part(0), ALU.subtract))
                link(nc.vector.tensor_copy(part(1), by_head(k_r1)))
                link(nc.vector.tensor_tensor(by_head(k_r2), by_head(k_r1), part(1), ALU.subtract))
                nc.vector.tensor_copy(part(2), by_head(k_r2)).then_inc(k_rep_ready, 1)
                dve.wait_ge(kT_psum, k + 1)
                nc.vector.tensor_copy(kT[:, :, k * P:(k + 1) * P].bitcast(i32), turned[:, :, :].bitcast(i32)) \
                    .then_inc(kT_ready, 1)

            first_stats((None, 0))
            after(dve, bn1_done, (None, 0))
            first_norm((None, 0))

            for c in range(DC):
                dve.wait_ge(v_psum, c + 1)
                nc.vector.tensor_scalar(vb[:, c, :], scores[0][:, c, :], bv_sb[:, c:c + 1], 0.0, ALU.add, ALU.add) \
                    .then_inc(v_read, 1)
                dve.wait_ge(v_read, c + 1)
                nc.vector.tensor_reduce(v_max[:, c:c + 1], vb[:, c, :], axis=AX.X, op=ALU.max,
                                        apply_absolute_value=True).then_inc(v_chain, 1)
            dve.wait_ge(v_chain, 2)
            nc.vector.tensor_scalar(v_step[:, :], v_max[:, :], 1.0 / 127.0, S_EPS, ALU.mult, ALU.max) \
                .then_inc(v_chain, 1)
            dve.wait_ge(v_chain, 3)
            nc.vector.reciprocal(v_inv[:, :], v_step[:, :]).then_inc(v_chain, 1)
            dve.wait_ge(v_chain, 4)
            for c in range(DC):
                nc.vector.tensor_scalar(v_s[:, c, :], vb[:, c, :], v_inv[:, c:c + 1], MAGIC, ALU.mult, ALU.add) \
                    .then_inc(v_chain, 1)
                dve.wait_ge(v_chain, 5 + c)
                nc.vector.tensor_scalar(v_i[:, c, :], v_s[:, c, :], MAGIC, 0.0, ALU.subtract, ALU.add) \
                    .then_inc(v_int_ready, 1)
            queries((None, 0))
            query_parts((None, 0))
            for c in range(DC):
                dve.wait_ge(V_psum, c + 1)
                nc.vector.tensor_copy(V[:, :, c * P:(c + 1) * P], turned[:, 0:KC, :]).then_inc(V_ready, 1)
            qT_copy((None, 0))
            first_stats((None, 1))
            after(dve, bn1_done, (None, 1))
            first_norm((None, 1))
            dve.wait_ge(got_proj, 32)
            for c in range(DC):
                nc.vector.tensor_scalar(wp_sb[:, c, :], wp_raw[:, c, :], v_step[:, c:c + 1], 0.0, ALU.mult, ALU.add) \
                    .then_inc(wp_ready, 1)
            maxima((None, 0), 0)
            maxima((None, 0), 1)

            def weight_steps():
                dve.wait_ge(w_sum_psum, 1)
                nc.vector.tensor_scalar(w_step[:, :, :].rearrange("p m e -> p (m e)"), ffn[:, 0:3 * EXPERTS],
                                        1.0 / (D * D), Q_EPS, ALU.mult, ALU.max).then_inc(w_step_ready, 1)
                dve.wait_ge(w_step_ready, 1)
                nc.vector.reciprocal(w_inv[:, :, :], w_step[:, :, :]).then_inc(w_step_ready, 1)
                nc.vector.tensor_tensor(tab_t[:, :], w_step[:, 0, :], w_step[:, 0, :], ALU.mult).then_inc(w_chain, 1)
                dve.wait_ge(w_chain, 1)
                nc.vector.tensor_tensor(tab[:, 0, :], tab_t[:, :], w_step[:, 1, :], ALU.mult).then_inc(w_chain, 1)
                nc.vector.tensor_scalar(tab[:, 1, :], w_step[:, 2, :], 1.0 / 127.0, 0.0, ALU.mult, ALU.add) \
                    .then_inc(w_chain, 1)

            def weights_ternary(n):
                m, e = n % 3, n // 3
                w = gu_raw[:, :, e, m, :] if m < 2 else dn_raw[:, :, e, :]
                to = gu_w[:, :, e, m, :] if m < 2 else dn_w[:, :, e, :]
                dve.wait_ge(w_scaled, n + 1)
                nc.vector.tensor_scalar(w, w, MAGIC + 1.0, MAGIC - 1.0, ALU.min, ALU.max).then_inc(w_clipped, 1)
                dve.wait_ge(w_clipped, n + 1)
                nc.vector.tensor_scalar(to, w, MAGIC, 0.0, ALU.subtract, ALU.add).then_inc(w_ready, 1)

            def heads_normalised(t):
                after(dve, exp_done, t)
                nc.vector.reciprocal(rz[:, :], z[:, parity(t), :]).then_inc(rz_done.sem, 1)
                after(dve, rz_done, t)
                after(dve, pv_done, t)
                after(dve, attnT_psum, shift(t, -1))
                nc.vector.tensor_tensor(by_head(attn), heads_out[:, 0:D].rearrange("p (h d) -> p h d", d=HD),
                                        spread(rz), ALU.mult).then_inc(attn_done.sem, 1)

            def residual_and_norm(t):
                s = x2[:, parity(t), :]
                arrived(dve, x_res_in, t)
                nc.vector.tensor_tensor(xb[:, :], x_res[:, parity(t), :], bp_sb[:, :], ALU.add) \
                    .then_inc(xb_done.sem, 1)
                after(dve, xb_done, t)
                after(dve, proj_psum, t)
                nc.vector.tensor_tensor(s, front[:, 0:D], xb[:, :], ALU.add).then_inc(x2_done.sem, 1)
                after(dve, x2_done, t)
                nc.vector.bn_stats(bn2[:, :], s).then_inc(bn2_done.sem, 1)

            def second_aggregate(t):
                nc.vector.bn_aggr(mv2[:, :], bn2[:, :]).then_inc(mv2_done.sem, 1)

            def second_norm(t):
                after(dve, rstd2_done, t)
                nc.vector.tensor_scalar(ln2[:, :], x2[:, parity(t), :], mv2[:, 0:1], rstd2[:, :],
                                        ALU.subtract, ALU.mult).then_inc(ln2_done.sem, 1)

            def quantise_input(t):
                after(dve, ln2_done, t)
                nc.vector.tensor_reduce(a_max[:, :], ln2[:, :], axis=AX.X, op=ALU.max,
                                        apply_absolute_value=True).then_inc(a_chain.sem, 1)
                after(dve, a_chain, t, 1)
                after(dve, c_chain, shift(t, -1))
                nc.vector.tensor_scalar(a_step[:, :], a_max[:, :], 1.0 / 127.0, Q_EPS / 127.0,
                                        ALU.mult, ALU.max).then_inc(a_chain.sem, 1)
                after(dve, a_chain, t, 2)
                nc.vector.reciprocal(a_inv[:, :], a_step[:, :]).then_inc(a_chain.sem, 1)
                after(dve, a_chain, t, 3)
                after(dve, a_q_done, shift(t, -1))
                nc.vector.tensor_scalar(a_m[:, :], ln2[:, :], a_inv[:, :], MAGIC, ALU.mult, ALU.add) \
                    .then_inc(a_chain.sem, 1)

            def route(t):
                after(dve, logits_psum, t)
                nc.vector.tensor_reduce(l_max[:, :], front[:, 0:EXPERTS], axis=AX.X, op=ALU.max) \
                    .then_inc(l_chain.sem, 1)
                after(dve, l_chain, t, 1)
                nc.vector.scalar_tensor_tensor(out=l_rank[:, :], in0=front[:, 0:EXPERTS], scalar=l_max[:, :],
                                               in1=order[:, :], op0=ALU.is_equal, op1=ALU.mult) \
                    .then_inc(l_chain.sem, 1)
                after(dve, l_chain, t, 2)
                nc.vector.tensor_reduce(l_top[:, :], l_rank[:, :], axis=AX.X, op=ALU.max).then_inc(l_chain.sem, 1)
                after(dve, l_chain, t, 3)
                after(dve, maskT_psum, shift(t, -1))
                nc.vector.tensor_scalar(mask[:, :], l_rank[:, :], l_top[:, :], 1.0, ALU.is_equal, ALU.mult) \
                    .then_inc(mask_done.sem, 1)
                after(dve, mask_done, t)
                nc.vector.tensor_tensor(sel_t[:, :, :], mask[:, :].unsqueeze(1).broadcast_to([P, 2, EXPERTS]),
                                        tab[:, :, :], ALU.mult).then_inc(sel_chain.sem, 1)
                after(dve, sel_chain, t)
                nc.vector.tensor_reduce(sel[:, parity(t), :], sel_t[:, :, :], axis=AX.X, op=ALU.add) \
                    .then_inc(sel_done.sem, 1)

            def aT_copy(t):
                after(dve, aT_psum, t)
                nc.vector.tensor_copy(aT[:, :, :].bitcast(i32), front_b[:, 0:DC, :].bitcast(i32)) \
                    .then_inc(aT_done.sem, 1)

            def maskT_copy(t):
                after(dve, maskT_psum, t)
                after(dve, hm_done, shift(t, -1))
                nc.vector.tensor_copy(maskT[:, :, :].bitcast(i32), ffn_b.bitcast(i32)).then_inc(maskT_done.sem, 1)

            def by_expert(t, to, src, src_done, done, free):
                after(dve, maskT_done, t)
                after(dve, src_done, t)
                after(dve, free, shift(t, -1))
                for c in range(DC):
                    nc.vector.tensor_tensor(to[:, c, :, :], maskT[:, :, :],
                                            src[:, c, :].unsqueeze(1).broadcast_to([P, EXPERTS, P]),
                                            ALU.mult).then_inc(done.sem, 1)

            def hidden(t):
                after(dve, relu_done, t)
                nc.vector.tensor_tensor(gu[:, :], g_relu[:, :], ffn[:, D:2 * D], ALU.mult).then_inc(gu_done.sem, 1)
                after(dve, gu_done, t)
                nc.vector.tensor_tensor(h[:, :], gu[:, :], g_relu[:, :], ALU.mult).then_inc(h_done.sem, 1)
                after(dve, h_done, t)
                nc.vector.tensor_reduce(h_max[:, :], h[:, :], axis=AX.X, op=ALU.max, apply_absolute_value=True) \
                    .then_inc(h_chain.sem, 1)
                after(dve, h_chain, t, 1)
                after(dve, h_scale_done, t)
                after(dve, y_scale_done, shift(t, -1))
                scale = h_scale[:, parity(t), :]
                nc.vector.tensor_scalar(h_abs[:, :], h_max[:, :], scale, Q_EPS, ALU.mult, ALU.max) \
                    .then_inc(h_chain.sem, 1)
                after(dve, h_chain, t, 2)
                nc.vector.reciprocal(h_inv[:, :], h_abs[:, :]).then_inc(h_chain.sem, 1)
                after(dve, h_chain, t, 3)
                nc.vector.tensor_scalar(h_mul[:, :], h_inv[:, :], scale, 127.0, ALU.mult, ALU.mult) \
                    .then_inc(h_chain.sem, 1)
                after(dve, h_chain, t, 4)
                after(dve, h_q_done, shift(t, -1))
                nc.vector.tensor_scalar(h_m[:, :], h[:, :], h_mul[:, :], MAGIC, ALU.mult, ALU.add) \
                    .then_inc(h_m_done.sem, 1)

            def result(t):
                after(dve, y_psum, t)
                after(dve, y_scale_done, t)
                p = parity(t)
                arrived(dve, y_out, t)
                nc.vector.scalar_tensor_tensor(out=y[:, p, :], in0=ffn[:, 0:D], scalar=y_scale[:, :],
                                               in1=x2[:, p, :], op0=ALU.mult, op1=ALU.add).then_inc(y_done.sem, 1)

            def tile_work(t):
                ahead, back, ffn1, ffn2 = shift(t, 1), shift(t, -1), shift(t, -2), shift(t, -3)
                for u in range(PAIRS):
                    if u == 4 and exists(back):
                        after(dve, bn2_done, back)
                    maxima(t, u + 2)
                    if u == 4 and exists(back):
                        second_aggregate(back)
                    if u == 0 and exists(back):
                        heads_normalised(back)
                    if number(t) == 0 and u == 0:
                        weight_steps()
                    if u == 0 and exists(ffn2):
                        by_expert(ffn2, hm, hT, hT_done, hm_done, y_psum)
                    if u == 0 and exists(ffn1):
                        maskT_copy(ffn1)
                    if u == 1 and exists(ffn1):
                        by_expert(ffn1, am, aT, aT_done, am_done, gu_psum)
                    if u == 1 and exists(ahead):
                        queries(ahead)
                        query_parts(ahead)
                    if u == 2 and exists(ffn2):
                        result(ffn2)
                    if u == 3 and exists(back):
                        residual_and_norm(back)
                    if u == 4 and exists(back):
                        second_norm(back)
                    if u == 4 and exists(ahead):
                        qT_copy(ahead)
                    if u == 4 and exists(back):
                        quantise_input(back)
                    if u == 6 and exists(back):
                        route(back)
                    if u == 6 and exists(ffn1):
                        hidden(ffn1)
                    if u == 7 and exists(shift(t, 2)):
                        first_stats(shift(t, 2))
                        after(dve, bn1_done, shift(t, 2))
                    if u == 7 and exists(back):
                        aT_copy(back)
                    if u == 7 and exists(shift(t, 2)):
                        first_norm(shift(t, 2))
                    if t[0] is None and t[1] < 2 and 1 <= 8 * t[1] + u < 13:
                        n = 2 * (8 * t[1] + u - 1)
                        weights_ternary(n)
                        weights_ternary(n + 1)

            run(dve, tile_work)

        @block.tensor
        def _(pe):
            def product(to, lhs, rhs, what=None):
                for c in range(DC):
                    last = nc.tensor.matmul(to, lhs(c), rhs(c), start=(c == 0), stop=(c == DC - 1))
                return last

            def turn_norm(t, ln, done, psum):
                after(pe, done, t)
                for c in range(DC):
                    last = nc.tensor.transpose(front[:, c * P:(c + 1) * P], ln[:, c * P:(c + 1) * P], ident[:, :])
                last.then_inc(psum.sem, 1)

            def queries(t):
                after(pe, lnT1_done, t)
                product(front[:, 0:D], lambda c: lnT1[:, c, :], lambda c: wq_sb[:, c, :]).then_inc(q_psum.sem, 1)

            def turn_queries(t):
                after(pe, q_rep_done, t)
                for p in range(PAIRS):
                    last = nc.tensor.transpose(front_b[:, p, :],
                                               q_rep[:, 2 * p:2 * p + 2, :].rearrange("p h s -> p (h s)"),
                                               ident_b[:, :])
                last.then_inc(qT_psum.sem, 1)

            def score(t, pair):
                t, pair = unit(t, pair)
                if not exists(t):
                    return
                if pair == 0:
                    after(pe, qT_done, t)
                before, b_pair = unit(t, pair - 2)
                for j in range(2):
                    after(pe, exp_done, before, 2 * b_pair + j + 1)
                    r = slice(j * SLOT, j * SLOT + ROWS)
                    last = nc.tensor.matmul(scores[pair % 2][:, j, :], qT[r, parity(t), pair, :],
                                            kT[r, pair, :], start=True, stop=True)
                last.then_inc(scores_done.sem, 1)

            def turn_probs(t, pair):
                after(pe, exp_done, t, 2 * pair + 2)
                before, b_pair = unit(t, pair - 1)
                after(pe, probsT_done, before, b_pair + 1)
                for j in range(2):
                    for k in range(KC):
                        last = nc.tensor.transpose(turned[:, j * KC + k, :],
                                                   probs[:, pair % 2, j, k * P:(k + 1) * P], ident_h[:, :])
                last.then_inc(turned_done.sem, 1)

            def values(t, pair):
                t, pair = unit(t, pair)
                if not exists(t):
                    return
                if pair == 0:
                    after(pe, attn_done, shift(t, -1))
                    for k in range(KC):
                        nc.tensor.matmul(heads_out[:, 0:D], minus_off[:, :], V[:, k, :], start=(k == 0), stop=False)
                after(pe, probsT_done, t, pair + 1)
                for j in range(2):
                    hd = 2 * pair + j
                    for k in range(KC):
                        last = nc.tensor.matmul(heads_out[:, hd * HD:(hd + 1) * HD], probsT[:, pair % 2, j * KC + k, :],
                                                V[:, k, hd * HD:(hd + 1) * HD], start=False,
                                                stop=(hd == HEADS - 1 and k == KC - 1))
                last.then_inc(pv_done.sem, 1)

            pe.wait_ge(got_kv, 64)
            pe.wait_ge(consts_ready, 1)
            pe.wait_ge(idents_ready, 3)

            def key_product(k):
                bank = ffn if k % 2 == 0 else heads_out
                if k >= 2:
                    pe.wait_ge(k_read, k - 1)
                product(bank[:, 0:D], lambda c: ctxT[:, c, k * P:(k + 1) * P], lambda c: wkv_sb[:, c, 0:D]) \
                    .then_inc(k_psum, 1)

            key_product(0)
            key_product(1)
            for c in range(DC):
                product(scores[0][:, c, :], lambda i: wkv_sb[:, i, D + c * P:D + (c + 1) * P],
                        lambda i: ctxT[:, i, :]).then_inc(v_psum, 1)
            for k in range(KC):
                if k + 2 < KC:
                    key_product(k + 2)
                pe.wait_ge(k_rep_ready, k + 1)
                if k:
                    pe.wait_ge(kT_ready, k)
                for p in range(PAIRS):
                    last = nc.tensor.transpose(turned[:, p, :].bitcast(bf16),
                                               k_rep[:, 2 * p:2 * p + 2, :].rearrange("p h s -> p (h s)"),
                                               ident_b[:, :])
                last.then_inc(kT_psum, 1)
            turn_norm((None, 0), ln1, ln1_done, lnT1_psum)
            pe.wait_ge(got_front, 32)
            queries((None, 0))
            pe.wait_ge(kT_ready, KC)
            for c in range(DC):
                pe.wait_ge(v_int_ready, c + 1)
                if c:
                    pe.wait_ge(V_ready, c)
                for k in range(KC):
                    last = nc.tensor.transpose(turned[:, k, :], v_i[:, c, k * P:(k + 1) * P], ident_h[:, :])
                last.then_inc(V_psum, 1)
            turn_queries((None, 0))
            pe.wait_ge(V_ready, DC)
            pe.wait_ge(wp_ready, DC)
            score((None, 0), 0)
            score((None, 0), 1)
            pe.wait_ge(w_abs_ready, 3 * EXPERTS)
            nc.tensor.matmul(ffn[:, 0:3 * EXPERTS], ones[:, :], w_abs[:, :, :].rearrange("p m e -> p (m e)"),
                             start=True, stop=True).then_inc(w_sum_psum, 1)

            def gate_up(t, quarter):
                if quarter == 0:
                    if t[0] is None and t[1] == 0:
                        pe.wait_ge(w_ready, 3 * EXPERTS)
                    after(pe, am_done, t)
                    after(pe, y_done, shift(t, -1))
                for i in range(4 * quarter, 4 * quarter + 4):
                    c, e = i // EXPERTS, i % EXPERTS
                    last = nc.tensor.matmul(ffn[:, :], am[:, c, e, :], gu_w[:, c, e, :, :].rearrange("p a n -> p (a n)"),
                                            start=(i == 0), stop=(i == DC * EXPERTS - 1))
                if quarter == 3:
                    last.then_inc(gu_psum.sem, 1)

            def down(t, half):
                if half == 0:
                    after(pe, hm_done, t)
                    after(pe, maskT_done, shift(t, 1))
                for i in range(8 * half, 8 * half + 8):
                    c, e = i // EXPERTS, i % EXPERTS
                    last = nc.tensor.matmul(ffn[:, 0:D], hm[:, c, e, :], dn_w[:, c, e, :],
                                            start=(i == 0), stop=(i == DC * EXPERTS - 1))
                if half == 1:
                    last.then_inc(y_psum.sem, 1)

            def tile_work(t):
                ahead, back, ffn1, ffn2 = shift(t, 1), shift(t, -1), shift(t, -2), shift(t, -3)
                for u in range(PAIRS):
                    score(t, u + 2)
                    if exists(t):
                        turn_probs(t, u)
                    values(t, u - 1)
                    if u == 0:
                        if exists(ahead):
                            after(pe, aT_done, shift(t, -2))
                            after(pe, qT_done, t)
                            turn_norm(ahead, ln1, ln1_done, lnT1_psum)
                        if exists(ffn2):
                            after(pe, aT_done, shift(t, -2))
                            after(pe, h_q_done, ffn2)
                            for c in range(DC):
                                last = nc.tensor.transpose(front_b[:, 2 * DC + c, :], h_q[:, c * P:(c + 1) * P],
                                                           ident_b[:, :])
                            last.then_inc(hT_psum.sem, 1)
                        if exists(ffn1):
                            after(pe, mask_done, ffn1)
                            after(pe, gu_done, ffn2)
                            for e in range(EXPERTS):
                                last = nc.tensor.transpose(ffn_b[:, e, :], mask[:, e:e + 1].broadcast_to([P, P]),
                                                           ident_b[:, :])
                            last.then_inc(maskT_psum.sem, 1)
                    if u == 1:
                        if exists(ahead):
                            if exists(ffn2):
                                after(pe, hT_done, ffn2)
                            queries(ahead)
                        if exists(ffn2):
                            down(ffn2, 0)
                    if u == 2:
                        if exists(back):
                            if exists(ahead):
                                after(pe, qb_done, ahead)
                            if exists(ffn2):
                                after(pe, hT_done, ffn2)
                            turn_norm(back, attn, attn_done, attnT_psum)
                        if exists(ffn2):
                            down(ffn2, 1)
                    if u == 3 and exists(back):
                        after(pe, attnT_done, back)
                        product(front[:, 0:D], lambda c: attnT[:, c, :], lambda c: wp_sb[:, c, :]) \
                            .then_inc(proj_psum.sem, 1)
                    if u == 4 and exists(ahead):
                        if exists(back):
                            after(pe, x2_done, back)
                        turn_queries(ahead)
                    if u == 5 and exists(back):
                        if exists(ahead):
                            after(pe, qT_done, ahead)
                        turn_norm(back, ln2, ln2_done, lnT2_psum)
                    if u == 6 and exists(back):
                        if number(back) == 0:
                            pe.wait_ge(got_router, 16)
                        after(pe, lnT2_done, back)
                        product(front[:, 0:EXPERTS], lambda c: lnT2[:, c, :], lambda c: rT[:, c, :]) \
                            .then_inc(logits_psum.sem, 1)
                    if 3 <= u <= 6 and exists(ffn1):
                        gate_up(ffn1, u - 3)
                    if u == 7 and exists(back):
                        after(pe, l_chain, back, 2)
                        after(pe, a_q_done, back)
                        for c in range(DC):
                            last = nc.tensor.transpose(front_b[:, c, :], a_q[:, c * P:(c + 1) * P], ident_b[:, :])
                        last.then_inc(aT_psum.sem, 1)

            run(pe, tile_work)


def kernel(**inputs):
    import numpy as np
    import concourse.bacc as bacc
    from concourse.bass_utils import run_bass_kernel_spmd

    a = {k: np.asarray(v) for k, v in inputs.items()}
    batch, tokens, dim = a["x"].shape
    experts = a["L0_ffn_router_w"].shape[0]
    chunks = dim // 128

    def by_chunk(w):
        return w.transpose(2, 0, 1).reshape(chunks, 128, experts, -1)

    laid = {
        "x": a["x"].reshape(batch * tokens, dim),
        "ctx_t": a["ctx_2048"].reshape(-1, dim).T,
        "wq": a["L0_xattn_Wq"],
        "bq": a["L0_xattn_bq"].reshape(1, dim),
        "wkv": a["L0_xattn_Wkv"],
        "bk": a["L0_xattn_bkv"][:dim].reshape(1, dim),
        "bv": a["L0_xattn_bkv"][dim:].reshape(chunks, 128).T,
        "wp": a["L0_xattn_Wp"],
        "bp": a["L0_xattn_bp"].reshape(1, dim),
        "router": a["L0_ffn_router_w"].T.reshape(chunks, 128, experts),
        "w_gate_up": np.stack([by_chunk(a["L0_ffn_wg"]), by_chunk(a["L0_ffn_wu"])], axis=3),
        "w_down": by_chunk(a["L0_ffn_wd"]),
    }
    nc = bacc.Bacc("TRN2", target_bir_lowering=False, num_devices=1)
    arrays, args = {}, []
    for name, v in laid.items():
        v = np.ascontiguousarray(v)
        arrays[f"in_{name}"] = v
        args.append(nc.dram_tensor(f"in_{name}", v.shape, mybir.dt.from_np(v.dtype), kind="ExternalInput").ap())
    out = nc.dram_tensor("out_x", (batch * tokens, dim), mybir.dt.float32, kind="ExternalOutput").ap()
    cross_attention_moe(nc, *args, out)
    r = run_bass_kernel_spmd(nc, [arrays], core_ids=[0])
    return r.results[0]["out_x"].reshape(batch, tokens, dim)
```

```python
import concourse.bass as bass
from concourse import mybir
from contextlib import ExitStack
import math


class Signal:

    def __init__(self, sem, per_tile):
        self.sem, self.per_tile = sem, per_tile

    def value(self, tile, nth):
        register, offset = tile
        fixed = self.per_tile * offset + nth
        return fixed if register is None else register * self.per_tile + fixed


def cross_attention_moe(nc, x, ctx_t, wq, wkv, wp, biases, router, w_gate_up, w_down, out):
    fp32, bf16, fp16 = mybir.dt.float32, mybir.dt.bfloat16, mybir.dt.float16
    u8, u16, i32 = mybir.dt.uint8, mybir.dt.uint16, mybir.dt.int32
    ALU = mybir.AluOpType
    ACT = mybir.ActivationFunctionType
    AX = mybir.AxisListType

    P = 128
    TOKENS, D = x.shape
    KEYS = ctx_t.shape[1]
    EXPERTS = router.shape[2]
    HEADS = 16
    HD = D // HEADS
    DC = D // P
    KC = KEYS // P
    TILES = TOKENS // P
    PAIRS = HEADS // 2
    PARTS = 3
    SLOT = 64
    ROWS = PARTS * HD
    RING = 4
    LAG = 2
    W_FROM, W_EACH = 7, 3
    MAGIC = 1.5 * 2.0 ** 23
    LEVELS = 255.0
    OFFSET = 1024.0
    LN_EPS = 1e-5
    Q_EPS = 1e-5
    S_EPS = 1e-8

    x_v = x.rearrange("(t p) c -> t p c", p=P)
    out_v = out.rearrange("(t p) c -> t p c", p=P)

    ctx = ExitStack()
    with ctx:
        def sb(name, shape, dt):
            return ctx.enter_context(nc.sbuf_tensor(name, shape, dt))

        def pb(name, shape, dt):
            return ctx.enter_context(nc.psum_tensor(name, shape, dt))

        def sem(name):
            return ctx.enter_context(nc.semaphore(name))

        def signal(name, per_tile=1):
            return Signal(sem(name), per_tile)

        ctxT = sb("ctxT", [P, DC, KEYS], fp32)
        wq_sb = sb("wq_sb", [P, DC, D], fp32)
        wkv_sb = sb("wkv_sb", [P, DC, 2 * D], fp32)
        wp_raw = sb("wp_raw", [P, DC, D], fp32)
        wp_sb = sb("wp_sb", [P, DC, D], fp32)
        bias_row = sb("bias_row", [P, 4 * D], fp32)
        bias_r1 = sb("bias_r1", [P, 4 * D], fp32)
        bias_hi = sb("bias_hi", [P, 4 * D], bf16)
        bias_mid = sb("bias_mid", [P, 4 * D], bf16)
        bias3 = sb("bias3", [P, 4 * D], bf16)
        ones_b = sb("ones_b", [P, KEYS], bf16)
        rT = sb("rT", [P, DC, EXPERTS], fp32)
        gu_raw = sb("gu_raw", [P, DC, EXPERTS, 2, D], fp32)
        dn_raw = sb("dn_raw", [P, DC, EXPERTS, D], fp32)
        gu_w = sb("gu_w", [P, DC, EXPERTS, 2, D], bf16)
        dn_w = sb("dn_w", [P, DC, EXPERTS, D], bf16)
        w_abs = sb("w_abs", [P, 3, EXPERTS], fp32)
        w_scratch = sb("w_scratch", [P, DC, D], bf16)
        w_step = sb("w_step", [P, 3, EXPERTS], fp32)
        w_inv = sb("w_inv", [P, 3, EXPERTS], fp32)
        tab = sb("tab", [P, 2, EXPERTS], fp32)
        tab_t = sb("tab_t", [P, EXPERTS], fp32)
        ident = sb("ident", [P, P], fp32)
        ident_b = sb("ident_b", [P, P], bf16)
        ones = sb("ones", [P, P], fp32)
        minus_off = sb("minus_off", [P, P], fp16)
        minus_half = sb("minus_half", [P, 1], fp32)
        eps = sb("eps", [P, 1], fp32)
        ln_levels = sb("ln_levels", [P, 2], fp32)
        head_scale = sb("head_scale", [P, 2, HEADS], fp32)
        order = sb("order", [P, EXPERTS], fp32)
        kT = sb("kT", [P, PAIRS, KEYS], bf16)
        V = sb("V", [P, KC, D], fp16)

        k_max = sb("k_max", [P, KC, HEADS], fp32)
        k_step = sb("k_step", [P, KC, HEADS], fp32)
        k_inv = sb("k_inv", [P, KC, HEADS], fp32)
        k_s = sb("k_s", [P, KC, D], fp32)
        k_i = sb("k_i", [P, KC, D], fp32)
        k_q = sb("k_q", [P, KC, D], fp32)
        k_r1 = sb("k_r1", [P, KC, D], fp32)
        k_rep = sb("k_rep", [P, KC, HEADS, SLOT], bf16)
        v_max = sb("v_max", [P, DC], fp32)
        v_step = sb("v_step", [P, DC], fp32)
        v_inv = sb("v_inv", [P, DC], fp32)
        v_s = sb("v_s", [P, DC, KEYS], fp32)
        v_i = sb("v_i", [P, DC, KEYS], fp16)

        x_ln = sb("x_ln", [P, 2, D], fp32)
        x_res = sb("x_res", [P, 2, D], fp32)
        bn1 = sb("bn1", [P, 6], fp32)
        mv1 = sb("mv1", [P, 2], fp32)
        var1 = sb("var1", [P, 1], fp32)
        rstd1 = sb("rstd1", [P, 1], fp32)
        ln1 = sb("ln1", [P, D], fp32)
        lnT1 = sb("lnT1", [P, DC, P], fp32)
        q_max = sb("q_max", [P, HEADS], fp32)
        q_step = sb("q_step", [P, HEADS], fp32)
        q_inv = sb("q_inv", [P, HEADS], fp32)
        q_s = sb("q_s", [P, D], fp32)
        q_i = sb("q_i", [P, D], bf16)
        q_rep = sb("q_rep", [P, HEADS, SLOT // HD, HD], bf16)
        q_scale = sb("q_scale", [P, 2, HEADS], fp32)
        q_nscale = sb("q_nscale", [P, 2, HEADS], fp32)
        qT = sb("qT", [P, 2, PAIRS, P], bf16)
        s_max = sb("s_max", [P, 2, 2], fp32)
        nb0 = sb("nb0", [P, 2, 2], fp32)
        nb = sb("nb", [P, 2, 2], fp32)
        probs = sb("probs", [P, RING, 2, KEYS], fp16)
        probsT = sb("probsT", [P, RING, 2 * KC, P], fp16)
        z = sb("z", [P, 2, HEADS], fp32)
        rz = sb("rz", [P, HEADS], fp32)
        attn = sb("attn", [P, D], fp32)
        attnT = sb("attnT", [P, DC, P], fp32)
        x2 = sb("x2", [P, 2, D], fp32)
        bn2 = sb("bn2", [P, 6], fp32)
        mv2 = sb("mv2", [P, 2], fp32)
        var2 = sb("var2", [P, 1], fp32)
        rstd2 = sb("rstd2", [P, 1], fp32)
        ln2 = sb("ln2", [P, D], fp32)
        lnT2 = sb("lnT2", [P, DC, P], fp32)
        a_max = sb("a_max", [P, 1], fp32)
        a_step = sb("a_step", [P, 1], fp32)
        a_inv = sb("a_inv", [P, 1], fp32)
        a_m = sb("a_m", [P, D], fp32)
        a_q = sb("a_q", [P, D], bf16)
        aT = sb("aT", [P, DC, P], bf16)
        l_max = sb("l_max", [P, 1], fp32)
        l_rank = sb("l_rank", [P, EXPERTS], fp32)
        l_top = sb("l_top", [P, 1], fp32)
        mask = sb("mask", [P, EXPERTS], bf16)
        sel_t = sb("sel_t", [P, 2, EXPERTS], fp32)
        sel = sb("sel", [P, 2, 2], fp32)
        c1 = sb("c1", [P, 1], fp32)
        c2 = sb("c2", [P, 1], fp32)
        h_scale = sb("h_scale", [P, 2, 1], fp32)
        maskT = sb("maskT", [P, 2, EXPERTS, P], bf16)
        am = sb("am", [P, DC, EXPERTS, P], bf16)
        g_relu = sb("g_relu", [P, D], fp32)
        gu = sb("gu", [P, D], fp32)
        h = sb("h", [P, D], fp32)
        h_max = sb("h_max", [P, 1], fp32)
        h_abs = sb("h_abs", [P, 1], fp32)
        h_inv = sb("h_inv", [P, 1], fp32)
        h_mul = sb("h_mul", [P, 1], fp32)
        y_scale = sb("y_scale", [P, 1], fp32)
        h_m = sb("h_m", [P, D], fp32)
        h_q = sb("h_q", [P, D], bf16)
        hT = sb("hT", [P, DC, P], bf16)
        hm = sb("hm", [P, DC, EXPERTS, P], bf16)
        y = sb("y", [P, 2, D], fp32)

        scores = [pb(f"scores{i}", [P, 2, KEYS], fp32) for i in range(2)]
        heads_out = pb("heads_out", [P, 2 * D], fp32)
        front = pb("front", [P, 2 * D], fp32)
        back = pb("back", [P, 2 * D], fp32)
        ffn = pb("ffn", [P, 2 * D], fp32)
        front_b = front[:, :].bitcast(bf16).rearrange("p (n q) -> p n q", q=P)
        k_psum_v = scores[0][:, :, :].rearrange("p a (b n) -> p (a b) n", n=D)

        got_bias = sem("got_bias")
        got_kv = sem("got_kv")
        got_wq = sem("got_wq")
        got_wp = sem("got_wp")
        got_router = sem("got_router")
        got_experts = [sem(f"got_experts{e}") for e in range(EXPERTS)]
        zero_ready = sem("zero_ready")
        consts_ready = sem("consts_ready")
        idents_ready = sem("idents_ready")
        bias_chain = sem("bias_chain")
        bias_ready = sem("bias_ready")
        k_psum = sem("k_psum")
        k_read = sem("k_read")
        k_chain = sem("k_chain")
        k_rep_ready = sem("k_rep_ready")
        kT_ready = sem("kT_ready")
        v_psum = sem("v_psum")
        v_chain = sem("v_chain")
        v_int_ready = sem("v_int_ready")
        V_ready = sem("V_ready")
        wp_ready = sem("wp_ready")
        reached = {e: sem(f"reached_{e}") for e in ("sp", "pool", "dve")}
        w_abs_ready = sem("w_abs_ready")
        w_sum_psum = sem("w_sum_psum")
        w_step_ready = sem("w_step_ready")
        w_chain = sem("w_chain")
        w_scaled = sem("w_scaled")
        w_clipped = sem("w_clipped")
        w_ready = sem("w_ready")

        x_ln_in = [sem(f"x_ln_in{i}") for i in range(2)]
        x_res_in = [sem(f"x_res_in{i}") for i in range(2)]
        y_out = [sem(f"y_out{i}") for i in range(2)]
        bn1_done = signal("bn1_done")
        mv1_done = signal("mv1_done")
        var1_done = signal("var1_done")
        rstd1_done = signal("rstd1_done")
        ln1_done = signal("ln1_done")
        lnT1_psum = signal("lnT1_psum")
        lnT1_done = signal("lnT1_done")
        q_psum = signal("q_psum")
        q_chain = signal("q_chain", 4)
        q_scale_done = signal("q_scale_done", 2)
        q_i_done = signal("q_i_done")
        q_rep_done = signal("q_rep_done")
        qT_psum = signal("qT_psum")
        qT_done = signal("qT_done")
        scores_done = signal("scores_done", PAIRS)
        max_done = signal("max_done", PAIRS)
        nb0_done = signal("nb0_done", PAIRS)
        nb_done = signal("nb_done", PAIRS)
        exp_done = signal("exp_done", HEADS)
        probsT_done = [signal(f"probsT_done{i}", 16 * PAIRS // RING) for i in range(RING)]
        pv_done = signal("pv_done", PAIRS)
        rz_done = signal("rz_done")
        attn_done = signal("attn_done")
        attnT_psum = signal("attnT_psum")
        attnT_done = signal("attnT_done")
        proj_psum = signal("proj_psum")
        x2_done = signal("x2_done")
        bn2_done = signal("bn2_done")
        mv2_done = signal("mv2_done")
        var2_done = signal("var2_done")
        rstd2_done = signal("rstd2_done")
        ln2_done = signal("ln2_done")
        lnT2_psum = signal("lnT2_psum")
        lnT2_done = signal("lnT2_done")
        logits_psum = signal("logits_psum")
        a_chain = signal("a_chain", 4)
        a_q_done = signal("a_q_done")
        l_chain = signal("l_chain", 3)
        mask_done = signal("mask_done")
        sel_chain = signal("sel_chain")
        sel_done = signal("sel_done")
        c_chain = signal("c_chain", 2)
        h_scale_done = signal("h_scale_done")
        aT_done = signal("aT_done", 16)
        maskT_psum = signal("maskT_psum")
        maskT_done = signal("maskT_done")
        am_done = signal("am_done", DC)
        gu_psum = signal("gu_psum")
        relu_done = signal("relu_done")
        gu_done = signal("gu_done")
        h_done = signal("h_done")
        h_chain = signal("h_chain", 4)
        y_scale_done = signal("y_scale_done")
        h_m_done = signal("h_m_done")
        h_q_done = signal("h_q_done")
        hT_done = signal("hT_done", 16)
        hm_done = signal("hm_done", DC)
        y_psum = signal("y_psum")
        y_done = signal("y_done")

        def shift(tile, by):
            return tile[0], tile[1] + by

        def number(tile):
            return tile[1] if tile[0] is None else None

        def exists(tile):
            return tile[0] is not None or 0 <= tile[1] < TILES

        def unit(tile, pair):
            return shift(tile, pair // PAIRS), pair % PAIRS

        def after(eng, what, tile, nth=None):
            if not exists(tile):
                return
            eng.wait_ge(what.sem, what.value(tile, what.per_tile if nth is None else nth))

        def parity(tile):
            return tile[1] % 2

        LOOP_FROM, LOOP_TO = 4, TILES - 2
        ENDS = TILES + 3

        def run(eng, body):
            for t in range(LOOP_FROM):
                body((None, t))
            with eng.Fori(0, (LOOP_TO - LOOP_FROM) // 2) as turn:
                body((turn * 2, LOOP_FROM))
                body((turn * 2, LOOP_FROM + 1))
            for t in range(LOOP_TO, ENDS):
                body((None, t))

        block = ctx.enter_context(nc.Block())

        def carry(eng, name):
            eng.sem_inc(reached[name], 1)

        def arrived(eng, sems, t):
            p = parity(t)
            fixed = 8 * (t[1] - p) + 16
            eng.wait_ge(sems[p], fixed if t[0] is None else t[0] * 8 + fixed)

        def by_head(a):
            return a.rearrange("p (h d) -> p h d", d=HD)

        @block.sync
        def _(sp):
            def rows(v, t):
                return v[t[1]] if t[0] is None else v[t[0] + t[1]]

            def load(into, done, t):
                sp.dma_start(into[:, parity(t), :], rows(x_v, t)).then_inc(done[parity(t)], 16)

            sp.dma_start(bias_row[:, :], biases.broadcast_to([P, 4 * D])).then_inc(got_bias, 16)
            load(x_ln, x_ln_in, (None, 0))
            sp.dma_start(wkv_sb[:, :, :], wkv.rearrange("(c p) n -> p c n", p=P)).then_inc(got_kv, 16)
            load(x_ln, x_ln_in, (None, 1))
            sp.dma_start(wp_raw[:, :, :], wp.rearrange("(c p) n -> p c n", p=P)).then_inc(got_wp, 16)
            sp.dma_start(rT[:, :, :], router.rearrange("c p e -> p c e")).then_inc(got_router, 16)
            load(x_res, x_res_in, (None, 0))
            load(x_res, x_res_in, (None, 1))
            for k in range(KC):
                sp.wait_ge(k_rep_ready, k // 2 + 1)
                sp.dma_start_transpose(kT[:, :, k * P:(k + 1) * P], k_rep[:, k, :, :].rearrange("p h s -> p (h s)")) \
                    .then_inc(kT_ready, 16)
            for c in range(DC):
                sp.wait_ge(v_int_ready, c + 1)
                sp.dma_start_transpose(V[:, :, c * P:(c + 1) * P], v_i[:, c, :]).then_inc(V_ready, 16)

            def sp_after(what, tile, nth=None):
                if exists(tile):
                    after(sp, what, tile, nth)
                    carry(sp, "sp")

            def turn_probs(t, pair):
                sp_after(exp_done, t, 2 * pair + 2)
                before, b_pair = unit(t, pair - RING)
                sp_after(pv_done, before, b_pair + 1)
                sp.dma_start_transpose(probsT[:, pair % RING, :, :],
                                       probs[:, pair % RING, :, :].rearrange("p a k -> p (a k)")) \
                    .then_inc(probsT_done[pair % RING].sem, 16)

            def tile_work(t):
                back1, ffn1, ffn2 = shift(t, -1), shift(t, -2), shift(t, -3)
                for u in range(PAIRS):
                    if exists(t):
                        turn_probs(t, u)
                    if u == 0 and exists(shift(t, 2)):
                        sp_after(ln1_done, t)
                        load(x_ln, x_ln_in, shift(t, 2))
                    if u == 5 and exists(shift(t, 1)) and number(t) != 0:
                        sp_after(x2_done, back1)
                        load(x_res, x_res_in, shift(t, 1))
                    if u == 5 and exists(ffn2):
                        sp_after(y_done, ffn2)
                        sp.dma_start(rows(out_v, ffn2), y[:, parity(ffn2), :]).then_inc(y_out[parity(ffn2)], 16)
                    if u == 7 and exists(back1):
                        sp_after(a_q_done, back1)
                        sp_after(am_done, ffn1)
                        sp.dma_start_transpose(aT[:, :, :], a_q[:, :]).then_inc(aT_done.sem, 16)
                    if u == 1 and exists(ffn2):
                        sp_after(h_q_done, ffn2)
                        sp_after(hm_done, shift(ffn2, -1))
                        sp.dma_start_transpose(hT[:, :, :], h_q[:, :]).then_inc(hT_done.sem, 16)

            run(sp, tile_work)
            for i in range(2):
                sp.wait_ge(y_out[i], 16 * (TILES // 2 + 1))

        @block.scalar
        def _(act):
            act.dma_start(ctxT[:, :, :], ctx_t.rearrange("(c p) k -> p c k", p=P)).then_inc(got_kv, 16)
            act.dma_start(wq_sb[:, :, :], wq.rearrange("(c p) n -> p c n", p=P)).then_inc(got_wq, 16)
            act.wait_ge(got_kv, 32)
            for e in range(EXPERTS):
                act.dma_start(gu_raw[:, :, e, :, :], w_gate_up[:, :, e].rearrange("c p a n -> p c a n")) \
                    .then_inc(got_experts[e], 16)
                act.dma_start(dn_raw[:, :, e, :], w_down[:, :, e].rearrange("c p n -> p c n")) \
                    .then_inc(got_experts[e], 16)

            def weights_abs(e):
                act.wait_ge(got_experts[e], 32)
                for m in range(3):
                    w = gu_raw[:, :, e, m, :] if m < 2 else dn_raw[:, :, e, :]
                    if 3 * e + m:
                        act.wait_ge(w_abs_ready, 3 * e + m)
                    nc.scalar.activation(w_scratch[:, :, :], w, ACT.Abs,
                                         accum_out=w_abs[:, m, e:e + 1]).then_inc(w_abs_ready, 1)

            def from_psum(psum_ready, done, t, to, bank, func=ACT.Copy):
                after(act, psum_ready, t)
                nc.scalar.activation(to, bank, func).then_inc(done.sem, 1)

            def chunks(bank):
                return bank[:, 0:D].rearrange("p (c q) -> p c q", q=P)

            def exps(t, pair):
                t, pair = unit(t, pair)
                if not exists(t):
                    return
                after(act, nb_done, t, pair + 1)
                before, b_pair = unit(t, pair - RING)
                after(act, probsT_done[b_pair % RING], before, 16 * (b_pair // RING + 1))
                if pair == 0:
                    after(act, rz_done, shift(t, -2))
                i, s = pair % 2, pair % RING
                low = probs[:, s, :, :].rearrange("p a b -> p (a b)").bitcast(u8) \
                    .rearrange("p (a b two) -> p a b two", a=2, two=2)
                for j in range(2):
                    hd = 2 * pair + j
                    nc.scalar.activation(low[:, j, :, 0], scores[i][:, j, :], ACT.Exp,
                                         bias=nb[:, i, j:j + 1], scale=q_scale[:, parity(t), hd:hd + 1],
                                         accum_out=z[:, parity(t), hd:hd + 1]).then_inc(exp_done.sem, 1)

            from_psum(lnT1_psum, lnT1_done, (None, 0), lnT1[:, :, :], chunks(front))
            EARLY = 3
            for e in range(EARLY):
                weights_abs(e)
            from_psum(qT_psum, qT_done, (None, 0), qT[:, 0, :, :], front_b)
            act.wait_ge(consts_ready, 1)
            exps((None, 0), 0)

            def tile_work(t):
                ahead, back1, ffn1 = shift(t, 1), shift(t, -1), shift(t, -2)
                for u in range(PAIRS):
                    exps(t, u + 1)
                    if number(t) == 0 and EARLY + u < EXPERTS:
                        weights_abs(EARLY + u)
                    if u == 0 and exists(ahead):
                        from_psum(lnT1_psum, lnT1_done, ahead, lnT1[:, :, :], chunks(front))
                    if u == 2 and exists(back1):
                        from_psum(attnT_psum, attnT_done, back1, attnT[:, :, :], chunks(back))
                    if u == 4 and exists(ahead):
                        after(act, scores_done, back1)
                        from_psum(qT_psum, qT_done, ahead, qT[:, parity(ahead), :, :], front_b)
                    if u == 5 and exists(ffn1):
                        from_psum(gu_psum, relu_done, ffn1, g_relu[:, :], ffn[:, 0:D], ACT.Relu)
                    if u == 5 and exists(back1):
                        from_psum(lnT2_psum, lnT2_done, back1, lnT2[:, :, :], chunks(back))
                    if u == 7 and exists(back1):
                        after(act, hm_done, shift(t, -3))
                        from_psum(maskT_psum, maskT_done, back1, maskT[:, parity(back1), :, :], front_b)

            run(act, tile_work)

        @block.gpsimd
        def _(pool):
            pool.wait_ge(zero_ready, 1)
            nc.gpsimd.affine_select(out=ident[:, :], in_=ident[:, :], compare_op=ALU.not_equal, fill=1.0,
                                    base=0, pattern=[[-1, P]], channel_multiplier=1).then_inc(idents_ready, 1)

            def rstd(t, mv, mv_done, var, v_done, r, done):
                after(pool, mv_done, t)
                nc.gpsimd.tensor_tensor(var[:, :], mv[:, 1:2], eps[:, :], ALU.add).then_inc(v_done.sem, 1)
                after(pool, v_done, t)
                nc.gpsimd.tensor_tensor(r[:, :], var[:, :], minus_half[:, :], ALU.pow).then_inc(done.sem, 1)

            def bias(t, pair):
                t, pair = unit(t, pair)
                if not exists(t):
                    return
                i = pair % 2
                after(pool, max_done, t, pair + 1)
                if pair == 0:
                    after(pool, q_scale_done, t)
                before, b_pair = unit(t, pair - 2)
                after(pool, exp_done, before, 2 * b_pair + 2)
                nc.gpsimd.tensor_tensor(nb0[:, i, :], s_max[:, i, :],
                                        q_nscale[:, parity(t), 2 * pair:2 * pair + 2], ALU.mult) \
                    .then_inc(nb0_done.sem, 1)
                after(pool, nb0_done, t, pair + 1)
                nc.gpsimd.tensor_tensor(nb[:, i, :], nb0[:, i, :], ln_levels[:, :], ALU.add) \
                    .then_inc(nb_done.sem, 1)

            def q_scales(t):
                after(pool, q_chain, t, 2)
                after(pool, exp_done, shift(t, -2))
                for i, scaled in enumerate((q_nscale, q_scale)):
                    nc.gpsimd.tensor_tensor(scaled[:, parity(t), :], q_step[:, :], head_scale[:, i, :],
                                            ALU.mult).then_inc(q_scale_done.sem, 1)

            rstd((None, 0), mv1, mv1_done, var1, var1_done, rstd1, rstd1_done)
            rstd((None, 1), mv1, mv1_done, var1, var1_done, rstd1, rstd1_done)
            q_scales((None, 0))
            bias((None, 0), 0)
            bias((None, 0), 1)

            def weights_scaled(n):
                m, e = n % 3, n // 3
                w = gu_raw[:, :, e, m, :] if m < 2 else dn_raw[:, :, e, :]
                pool.wait_ge(w_step_ready, 2)
                nc.gpsimd.tensor_scalar(w, w, w_inv[:, m, e:e + 1], MAGIC, ALU.mult, ALU.add) \
                    .then_inc(w_scaled, 1)

            def tile_work(t):
                ahead, back1, ffn1 = shift(t, 1), shift(t, -1), shift(t, -2)
                for u in range(PAIRS):
                    bias(t, u + 2)
                    if t[0] is None and 0 <= 8 * t[1] + u - W_FROM < 3 * EXPERTS // W_EACH:
                        for n in range(W_EACH):
                            weights_scaled(W_EACH * (8 * t[1] + u - W_FROM) + n)
                    if u == 1 and exists(ahead):
                        q_scales(ahead)
                    if u == 3 and exists(back1):
                        rstd(back1, mv2, mv2_done, var2, var2_done, rstd2, rstd2_done)
                    if u == 5 and exists(back1):
                        after(pool, a_chain, back1, 4)
                        after(pool, aT_done, ffn1)
                        carry(pool, "pool")
                        nc.gpsimd.tensor_scalar(a_q[:, :], a_m[:, :], -MAGIC, 1.0, ALU.add, ALU.mult) \
                            .then_inc(a_q_done.sem, 1)
                        nc.gpsimd.tensor_tensor(c1[:, :], a_step[:, :], a_step[:, :], ALU.mult) \
                            .then_inc(c_chain.sem, 1)
                    if u == 7 and exists(back1):
                        after(pool, sel_done, back1)
                        nc.gpsimd.tensor_tensor(c2[:, :], a_step[:, :], sel[:, parity(back1), 0:1], ALU.mult) \
                            .then_inc(c_chain.sem, 1)
                        after(pool, c_chain, back1)
                        nc.gpsimd.tensor_tensor(h_scale[:, parity(back1), :], c1[:, :], c2[:, :], ALU.mult) \
                            .then_inc(h_scale_done.sem, 1)
                    if u == 3 and exists(shift(t, 2)):
                        rstd(shift(t, 2), mv1, mv1_done, var1, var1_done, rstd1, rstd1_done)
                    if u == 7 and exists(ffn1):
                        after(pool, h_m_done, ffn1)
                        after(pool, hT_done, shift(ffn1, -1))
                        carry(pool, "pool")
                        nc.gpsimd.tensor_scalar(h_q[:, :], h_m[:, :], -MAGIC, 1.0, ALU.add, ALU.mult) \
                            .then_inc(h_q_done.sem, 1)
                        after(pool, y_done, shift(ffn1, -1))
                        nc.gpsimd.tensor_tensor(y_scale[:, :], h_abs[:, :], sel[:, parity(ffn1), 1:2], ALU.mult) \
                            .then_inc(y_scale_done.sem, 1)

            run(pool, tile_work)

        @block.vector
        def _(dve):
            nc.vector.memset(ident[:, :], 0.0)
            nc.vector.memset(minus_half[:, :], -0.5)
            nc.vector.memset(eps[:, :], LN_EPS)
            nc.vector.memset(ln_levels[:, :], math.log(LEVELS))
            nc.vector.memset(head_scale[:, 0, :], -1.0 / math.sqrt(HD))
            nc.vector.memset(head_scale[:, 1, :], 1.0 / math.sqrt(HD)).then_inc(zero_ready, 1)
            nc.vector.memset(bias3[:, :].bitcast(fp32), 0.0)
            nc.vector.memset(ones_b[:, :], 1.0).then_inc(bias_chain, 1)
            n_bias = 1

            def link_bias(ins):
                nonlocal n_bias
                n_bias += 1
                ins.then_inc(bias_chain, 1)
                dve.wait_ge(bias_chain, n_bias)

            dve.wait_ge(bias_chain, 1)
            dve.wait_ge(got_bias, 16)
            link_bias(nc.vector.tensor_copy(bias_hi[:, :], bias_row[:, :]))
            nc.vector.tensor_copy(bias3[0:1, :], bias_hi[0:1, :]).then_inc(bias_ready, 1)
            link_bias(nc.vector.tensor_tensor(bias_r1[:, :], bias_row[:, :], bias_hi[:, :], ALU.subtract))
            link_bias(nc.vector.tensor_copy(bias_mid[:, :], bias_r1[:, :]))
            nc.vector.tensor_copy(bias3[32:33, :], bias_mid[32:33, :]).then_inc(bias_ready, 1)
            link_bias(nc.vector.tensor_tensor(bias_row[:, :], bias_r1[:, :], bias_mid[:, :], ALU.subtract))
            nc.vector.tensor_copy(bias3[64:65, :], bias_row[64:65, :]).then_inc(bias_ready, 1)

            def first_stats(t):
                arrived(dve, x_ln_in, t)
                nc.vector.bn_stats(bn1[:, :], x_ln[:, parity(t), :]).then_inc(bn1_done.sem, 1)

            def first_aggregate(t):
                after(dve, bn1_done, t)
                carry(dve, "dve")
                nc.vector.bn_aggr(mv1[:, :], bn1[:, :]).then_inc(mv1_done.sem, 1)

            def first_norm(t):
                after(dve, rstd1_done, t)
                after(dve, lnT1_psum, shift(t, -1))
                nc.vector.tensor_scalar(ln1[:, :], x_ln[:, parity(t), :], mv1[:, 0:1], rstd1[:, :],
                                        ALU.subtract, ALU.mult).then_inc(ln1_done.sem, 1)

            def query_steps(t):
                after(dve, q_psum, t)
                nc.vector.tensor_reduce(q_max[:, :], by_head(front[:, 0:D]), axis=AX.X,
                                        op=ALU.max, apply_absolute_value=True).then_inc(q_chain.sem, 1)
                after(dve, q_chain, t, 1)
                after(dve, q_scale_done, shift(t, -1))
                nc.vector.tensor_scalar(q_step[:, :], q_max[:, :], 1.0 / 127.0, S_EPS * math.sqrt(HD),
                                        ALU.mult, ALU.max).then_inc(q_chain.sem, 1)

            def query_inverse(t):
                after(dve, q_chain, t, 2)
                nc.vector.reciprocal(q_inv[:, :], q_step[:, :]).then_inc(q_chain.sem, 1)

            def query_scaled(t):
                after(dve, q_chain, t, 3)
                nc.vector.tensor_tensor(by_head(q_s[:, :]), by_head(front[:, 0:D]),
                                        q_inv[:, :].unsqueeze(2).broadcast_to([P, HEADS, HD]),
                                        ALU.mult).then_inc(q_chain.sem, 1)

            def query_rounded(t):
                after(dve, q_chain, t, 4)
                after(dve, q_rep_done, shift(t, -1))
                nc.vector.tensor_scalar(q_i[:, :], q_s[:, :], MAGIC, MAGIC, ALU.add, ALU.subtract) \
                    .then_inc(q_i_done.sem, 1)

            def query_copies(t):
                after(dve, q_i_done, t)
                after(dve, qT_psum, shift(t, -1))
                nc.vector.tensor_copy(q_rep[:, :, :, :],
                                      by_head(q_i[:, :]).unsqueeze(2).broadcast_to([P, HEADS, SLOT // HD, HD])) \
                    .then_inc(q_rep_done.sem, 1)

            def maxima(t, pair):
                t, pair = unit(t, pair)
                if not exists(t):
                    return
                after(dve, scores_done, t, pair + 1)
                nc.vector.tensor_reduce(s_max[:, pair % 2, :], scores[pair % 2][:, :, :], axis=AX.X, op=ALU.max) \
                    .then_inc(max_done.sem, 1)

            first_stats((None, 0))
            first_aggregate((None, 0))
            nc.vector.memset(ones[:, :], 1.0)
            nc.vector.memset(minus_off[:, :], -OFFSET)
            nc.vector.memset(k_rep[:, :, :, :].rearrange("p k h s -> p (k h s)").bitcast(fp32), 0.0)
            dve.wait_ge(idents_ready, 1)
            nc.vector.tensor_copy(ident_b[:, :], ident[:, :]).then_inc(idents_ready, 1)
            first_norm((None, 0))
            first_stats((None, 1))
            first_aggregate((None, 1))

            n_key = 0

            def link(ins):
                nonlocal n_key
                n_key += 1
                ins.then_inc(k_chain, 1)
                dve.wait_ge(k_chain, n_key)

            for i in range(KC // 2):
                k = slice(2 * i, 2 * i + 2)

                def heads_of(a):
                    return a[:, k, :].rearrange("p k (h d) -> p (k h) d", d=HD)

                def flat(a):
                    return a[:, k, :].rearrange("p k h -> p (k h)")

                def spread(a):
                    return flat(a).unsqueeze(2).broadcast_to([P, 2 * HEADS, HD])

                def part(j):
                    return k_rep[:, k, :, j * HD:(j + 1) * HD].rearrange("p k h d -> p (k h) d")

                dve.wait_ge(k_psum, 2 * i + 2)
                link(nc.vector.tensor_reduce(flat(k_max), heads_of(k_psum_v), axis=AX.X, op=ALU.max,
                                             apply_absolute_value=True))
                link(nc.vector.tensor_scalar(flat(k_step), flat(k_max), 1.0 / 127.0, S_EPS, ALU.mult, ALU.max))
                link(nc.vector.reciprocal(flat(k_inv), flat(k_step)))
                link(nc.vector.tensor_tensor(heads_of(k_s), heads_of(k_psum_v), spread(k_inv), ALU.mult))
                link(nc.vector.tensor_scalar(k_i[:, k, :], k_s[:, k, :], MAGIC, MAGIC, ALU.add, ALU.subtract))
                link(nc.vector.tensor_tensor(heads_of(k_q), heads_of(k_i), spread(k_step), ALU.mult))
                link(nc.vector.tensor_copy(part(0), heads_of(k_q)))
                link(nc.vector.tensor_tensor(heads_of(k_r1), heads_of(k_q), part(0), ALU.subtract))
                link(nc.vector.tensor_copy(part(1), heads_of(k_r1)))
                link(nc.vector.tensor_tensor(heads_of(k_s), heads_of(k_r1), part(1), ALU.subtract))
                nc.vector.tensor_copy(part(2), heads_of(k_s)).then_inc(k_rep_ready, 1)
                if i == 0:
                    first_norm((None, 1))
                    query_steps((None, 0))
                    query_inverse((None, 0))
                    query_scaled((None, 0))
                    query_rounded((None, 0))
                    query_copies((None, 0))

            for c in range(DC):
                dve.wait_ge(v_psum, c + 1)
                nc.vector.tensor_reduce(v_max[:, c:c + 1], scores[1][:, c, :], axis=AX.X, op=ALU.max,
                                        apply_absolute_value=True).then_inc(v_chain, 1)
            dve.wait_ge(v_chain, DC)
            nc.vector.tensor_scalar(v_step[:, :], v_max[:, :], 1.0 / 127.0, S_EPS, ALU.mult, ALU.max) \
                .then_inc(v_chain, 1)
            dve.wait_ge(v_chain, DC + 1)
            nc.vector.reciprocal(v_inv[:, :], v_step[:, :]).then_inc(v_chain, 1)
            dve.wait_ge(v_chain, DC + 2)
            for c in range(DC):
                nc.vector.tensor_scalar(v_s[:, c, :], scores[1][:, c, :], v_inv[:, c:c + 1], MAGIC,
                                        ALU.mult, ALU.add).then_inc(v_chain, 1)
            for c in range(DC):
                dve.wait_ge(v_chain, DC + 3 + c)
                nc.vector.tensor_scalar(v_i[:, c, :], v_s[:, c, :], MAGIC, 0.0, ALU.subtract, ALU.add) \
                    .then_inc(v_int_ready, 1)
            for i in range(RING // 2):
                nc.vector.memset(probs[:, 2 * i:2 * i + 2, :, :], OFFSET)
            for e in range(EXPERTS - 1):
                nc.vector.memset(order[:, e:e + 1], float(EXPERTS - e))
            nc.vector.memset(y[:, 0, :], 0.0).then_inc(y_out[0], 16)
            nc.vector.memset(y[:, 1, :], 0.0).then_inc(y_out[1], 16)
            nc.vector.memset(order[:, EXPERTS - 1:EXPERTS], 1.0).then_inc(consts_ready, 1)
            maxima((None, 0), 0)
            maxima((None, 0), 1)
            dve.wait_ge(got_wp, 16)
            for c in range(DC):
                nc.vector.tensor_scalar(wp_sb[:, c, :], wp_raw[:, c, :], v_step[:, c:c + 1], 0.0, ALU.mult, ALU.add) \
                    .then_inc(wp_ready, 1)

            def weight_steps():
                dve.wait_ge(w_sum_psum, 1)
                nc.vector.tensor_scalar(w_step[:, :, :].rearrange("p m e -> p (m e)"), ffn[:, 0:3 * EXPERTS],
                                        1.0 / (D * D), Q_EPS, ALU.mult, ALU.max).then_inc(w_step_ready, 1)
                dve.wait_ge(w_step_ready, 1)
                nc.vector.reciprocal(w_inv[:, :, :], w_step[:, :, :]).then_inc(w_step_ready, 1)
                nc.vector.tensor_tensor(tab_t[:, :], w_step[:, 0, :], w_step[:, 0, :], ALU.mult).then_inc(w_chain, 1)
                nc.vector.tensor_scalar(tab[:, 1, :], w_step[:, 2, :], 1.0 / 127.0, 0.0, ALU.mult, ALU.add) \
                    .then_inc(w_chain, 1)
                dve.wait_ge(w_chain, 2)
                nc.vector.tensor_tensor(tab[:, 0, :], tab_t[:, :], w_step[:, 1, :], ALU.mult).then_inc(w_chain, 1)

            def weights_ternary(n, count):
                def raw(i):
                    m, e = i % 3, i // 3
                    return gu_raw[:, :, e, m, :] if m < 2 else dn_raw[:, :, e, :]

                def made(i):
                    m, e = i % 3, i // 3
                    return gu_w[:, :, e, m, :] if m < 2 else dn_w[:, :, e, :]

                for i in range(n, n + count):
                    dve.wait_ge(w_scaled, i + 1)
                    nc.vector.tensor_scalar(raw(i), raw(i), MAGIC + 1.0, MAGIC - 1.0, ALU.min, ALU.max) \
                        .then_inc(w_clipped, 1)
                for i in range(n, n + count):
                    dve.wait_ge(w_clipped, i + 1)
                    nc.vector.tensor_scalar(made(i), raw(i), MAGIC, 0.0, ALU.subtract, ALU.add).then_inc(w_ready, 1)

            def sums_inverse(t):
                after(dve, exp_done, t)
                after(dve, attn_done, shift(t, -1))
                nc.vector.reciprocal(rz[:, :], z[:, parity(t), :]).then_inc(rz_done.sem, 1)

            def heads_normalised(t):
                after(dve, rz_done, t)
                after(dve, pv_done, t)
                after(dve, attnT_psum, shift(t, -1))
                nc.vector.tensor_tensor(by_head(attn[:, :]), by_head(heads_out[:, 0:D]),
                                        rz[:, :].unsqueeze(2).broadcast_to([P, HEADS, HD]), ALU.mult) \
                    .then_inc(attn_done.sem, 1)

            def residual(t):
                arrived(dve, x_res_in, t)
                after(dve, proj_psum, t)
                after(dve, y_done, shift(t, -2))
                nc.vector.tensor_tensor(x2[:, parity(t), :], back[:, 0:D], x_res[:, parity(t), :], ALU.add) \
                    .then_inc(x2_done.sem, 1)

            def second_stats(t):
                after(dve, x2_done, t)
                nc.vector.bn_stats(bn2[:, :], x2[:, parity(t), :]).then_inc(bn2_done.sem, 1)

            def second_aggregate(t):
                after(dve, bn2_done, t)
                carry(dve, "dve")
                nc.vector.bn_aggr(mv2[:, :], bn2[:, :]).then_inc(mv2_done.sem, 1)

            def second_norm(t):
                after(dve, rstd2_done, t)
                after(dve, lnT2_psum, shift(t, -1))
                nc.vector.tensor_scalar(ln2[:, :], x2[:, parity(t), :], mv2[:, 0:1], rstd2[:, :],
                                        ALU.subtract, ALU.mult).then_inc(ln2_done.sem, 1)

            def input_max(t):
                after(dve, ln2_done, t)
                nc.vector.tensor_reduce(a_max[:, :], ln2[:, :], axis=AX.X, op=ALU.max,
                                        apply_absolute_value=True).then_inc(a_chain.sem, 1)

            def input_step(t):
                after(dve, a_chain, t, 1)
                after(dve, h_scale_done, shift(t, -1))
                nc.vector.tensor_scalar(a_step[:, :], a_max[:, :], 1.0 / 127.0, Q_EPS / 127.0,
                                        ALU.mult, ALU.max).then_inc(a_chain.sem, 1)

            def input_inverse(t):
                after(dve, a_chain, t, 2)
                nc.vector.reciprocal(a_inv[:, :], a_step[:, :]).then_inc(a_chain.sem, 1)

            def input_scaled(t):
                after(dve, a_chain, t, 3)
                after(dve, a_q_done, shift(t, -1))
                nc.vector.tensor_scalar(a_m[:, :], ln2[:, :], a_inv[:, :], MAGIC, ALU.mult, ALU.add) \
                    .then_inc(a_chain.sem, 1)

            def logit_max(t):
                after(dve, logits_psum, t)
                nc.vector.tensor_reduce(l_max[:, :], back[:, 0:EXPERTS], axis=AX.X, op=ALU.max) \
                    .then_inc(l_chain.sem, 1)

            def logit_rank(t):
                after(dve, l_chain, t, 1)
                nc.vector.scalar_tensor_tensor(out=l_rank[:, :], in0=back[:, 0:EXPERTS], scalar=l_max[:, :],
                                               in1=order[:, :], op0=ALU.is_equal, op1=ALU.mult) \
                    .then_inc(l_chain.sem, 1)

            def logit_top(t):
                after(dve, l_chain, t, 2)
                nc.vector.tensor_reduce(l_top[:, :], l_rank[:, :], axis=AX.X, op=ALU.max).then_inc(l_chain.sem, 1)

            def expert_mask(t):
                after(dve, l_chain, t, 3)
                after(dve, maskT_psum, shift(t, -1))
                nc.vector.tensor_scalar(mask[:, :], l_rank[:, :], l_top[:, :], 1.0, ALU.is_equal, ALU.mult) \
                    .then_inc(mask_done.sem, 1)

            def expert_steps(t):
                after(dve, mask_done, t)
                nc.vector.tensor_tensor(sel_t[:, :, :], mask[:, :].unsqueeze(1).broadcast_to([P, 2, EXPERTS]),
                                        tab[:, :, :], ALU.mult).then_inc(sel_chain.sem, 1)

            def expert_select(t):
                after(dve, sel_chain, t)
                nc.vector.tensor_reduce(sel[:, parity(t), :], sel_t[:, :, :], axis=AX.X, op=ALU.add) \
                    .then_inc(sel_done.sem, 1)

            def by_expert(t, c, to, src, src_done, done, free):
                if c == 0:
                    after(dve, maskT_done, t)
                    after(dve, src_done, t)
                    after(dve, free, shift(t, -1))
                nc.vector.tensor_tensor(to[:, c, :, :], maskT[:, parity(t), :, :],
                                        src[:, c, :].unsqueeze(1).broadcast_to([P, EXPERTS, P]),
                                        ALU.mult).then_inc(done.sem, 1)

            def gate_up(t):
                after(dve, relu_done, t)
                after(dve, h_done, shift(t, -1))
                nc.vector.tensor_tensor(gu[:, :], g_relu[:, :], ffn[:, D:2 * D], ALU.mult).then_inc(gu_done.sem, 1)

            def hidden(t):
                after(dve, gu_done, t)
                after(dve, h_m_done, shift(t, -1))
                nc.vector.tensor_tensor(h[:, :], gu[:, :], g_relu[:, :], ALU.mult).then_inc(h_done.sem, 1)

            def hidden_max(t):
                after(dve, h_done, t)
                nc.vector.tensor_reduce(h_max[:, :], h[:, :], axis=AX.X, op=ALU.max, apply_absolute_value=True) \
                    .then_inc(h_chain.sem, 1)

            def hidden_abs(t):
                after(dve, h_chain, t, 1)
                after(dve, h_scale_done, t)
                after(dve, y_scale_done, shift(t, -1))
                nc.vector.tensor_scalar(h_abs[:, :], h_max[:, :], h_scale[:, parity(t), :], Q_EPS,
                                        ALU.mult, ALU.max).then_inc(h_chain.sem, 1)

            def hidden_inverse(t):
                after(dve, h_chain, t, 2)
                nc.vector.reciprocal(h_inv[:, :], h_abs[:, :]).then_inc(h_chain.sem, 1)

            def hidden_factor(t):
                after(dve, h_chain, t, 3)
                nc.vector.tensor_scalar(h_mul[:, :], h_inv[:, :], h_scale[:, parity(t), :], 127.0,
                                        ALU.mult, ALU.mult).then_inc(h_chain.sem, 1)

            def hidden_scaled(t):
                after(dve, h_chain, t, 4)
                after(dve, h_q_done, shift(t, -1))
                nc.vector.tensor_scalar(h_m[:, :], h[:, :], h_mul[:, :], MAGIC, ALU.mult, ALU.add) \
                    .then_inc(h_m_done.sem, 1)

            def result(t):
                after(dve, y_psum, t)
                after(dve, y_scale_done, t)
                arrived(dve, y_out, t)
                p = parity(t)
                nc.vector.scalar_tensor_tensor(out=y[:, p, :], in0=ffn[:, 0:D], scalar=y_scale[:, :],
                                               in1=x2[:, p, :], op0=ALU.mult, op1=ALU.add).then_inc(y_done.sem, 1)

            def tile_work(t):
                ahead, ahead2 = shift(t, 1), shift(t, 2)
                back1, ffn1, ffn2 = shift(t, -1), shift(t, -2), shift(t, -3)
                has_ahead, has_ahead2 = exists(ahead), exists(ahead2)
                has_back, has_ffn1, has_ffn2 = exists(back1), exists(ffn1), exists(ffn2)
                for u in range(PAIRS):
                    maxima(t, u + 2)
                    if u == 0:
                        if has_ffn1:
                            by_expert(ffn1, 0, am, aT, aT_done, am_done, gu_psum)
                            by_expert(ffn1, 1, am, aT, aT_done, am_done, gu_psum)
                    if u == 1:
                        if has_back:
                            sums_inverse(back1)
                        if has_ahead:
                            query_steps(ahead)
                        if has_back:
                            heads_normalised(back1)
                        if has_ahead:
                            query_inverse(ahead)
                        if has_ffn2:
                            by_expert(ffn2, 0, hm, hT, hT_done, hm_done, y_psum)
                    if u == 2:
                        if has_ahead:
                            query_scaled(ahead)
                        if has_ffn2:
                            by_expert(ffn2, 1, hm, hT, hT_done, hm_done, y_psum)
                        if has_ahead:
                            query_rounded(ahead)
                    if u == 3:
                        if has_ahead:
                            query_copies(ahead)
                        if has_ffn2:
                            result(ffn2)
                        if has_ahead2:
                            first_stats(ahead2)
                        if has_back:
                            residual(back1)
                        if has_ahead2:
                            first_aggregate(ahead2)
                        if has_back:
                            second_stats(back1)
                            second_aggregate(back1)
                    if u == 4:
                        if has_back:
                            second_norm(back1)
                        if has_ahead2:
                            first_norm(ahead2)
                        if has_back:
                            input_max(back1)
                    if u == 5:
                        if has_back:
                            input_step(back1)
                            input_inverse(back1)
                            input_scaled(back1)
                    if u == 6:
                        if has_ffn1:
                            gate_up(ffn1)
                        if has_back:
                            logit_max(back1)
                        if has_ffn1:
                            hidden(ffn1)
                        if has_back:
                            logit_rank(back1)
                        if has_ffn1:
                            hidden_max(ffn1)
                        if has_back:
                            logit_top(back1)
                        if has_ffn1:
                            hidden_abs(ffn1)
                        if has_back:
                            expert_mask(back1)
                    if u == 7:
                        if has_ffn1:
                            hidden_inverse(ffn1)
                        if has_back:
                            expert_steps(back1)
                        if has_ffn1:
                            hidden_factor(ffn1)
                        if has_back:
                            expert_select(back1)
                        if has_ffn1:
                            hidden_scaled(ffn1)
                    if t[0] is None and 8 * t[1] + u == W_FROM - 1:
                        weight_steps()
                    if t[0] is None and 0 <= 8 * t[1] + u - W_FROM < 3 * EXPERTS // W_EACH:
                        weights_ternary(W_EACH * (8 * t[1] + u - W_FROM), W_EACH)

            run(dve, tile_work)

        @block.tensor
        def _(pe):
            def add_bias(to, which):
                nc.tensor.matmul(to, ones_b[:, 0:P], bias3[:, which * D:(which + 1) * D], start=True, stop=False)

            def product(to, lhs, rhs, biased=False):
                for c in range(DC):
                    last = nc.tensor.matmul(to, lhs(c), rhs(c), start=(c == 0 and not biased), stop=(c == DC - 1))
                return last

            def turn_norm(t, bank, ln, done, psum):
                after(pe, done, t)
                for c in range(DC):
                    last = nc.tensor.transpose(bank[:, c * P:(c + 1) * P], ln[:, c * P:(c + 1) * P], ident[:, :])
                last.then_inc(psum.sem, 1)

            def queries(t):
                after(pe, lnT1_done, t)
                add_bias(front[:, 0:D], 0)
                product(front[:, 0:D], lambda c: lnT1[:, c, :], lambda c: wq_sb[:, c, :], biased=True) \
                    .then_inc(q_psum.sem, 1)

            def turn_queries(t):
                after(pe, q_rep_done, t)
                for p in range(PAIRS):
                    last = nc.tensor.transpose(front_b[:, p, :],
                                               q_rep[:, 2 * p:2 * p + 2, :, :].rearrange("p h r d -> p (h r d)"),
                                               ident_b[:, :])
                last.then_inc(qT_psum.sem, 1)

            def score(t, pair):
                t, pair = unit(t, pair)
                if not exists(t):
                    return
                if pair == 0:
                    after(pe, qT_done, t)
                before, b_pair = unit(t, pair - 2)
                for j in range(2):
                    after(pe, exp_done, before, 2 * b_pair + j + 1)
                    r = slice(j * SLOT, j * SLOT + ROWS)
                    last = nc.tensor.matmul(scores[pair % 2][:, j, :], qT[r, parity(t), pair, :],
                                            kT[r, pair, :], start=True, stop=True)
                last.then_inc(scores_done.sem, 1)

            def values(t, pair):
                t, pair = unit(t, pair)
                if not exists(t):
                    return
                if pair == 0:
                    after(pe, attn_done, shift(t, -1))
                    for k in range(KC):
                        nc.tensor.matmul(heads_out[:, 0:D], minus_off[:, :], V[:, k, :], start=(k == 0), stop=False)
                after(pe, probsT_done[pair % RING], t, 16 * (pair // RING + 1))
                for j in range(2):
                    hd = 2 * pair + j
                    for k in range(KC):
                        last = nc.tensor.matmul(heads_out[:, hd * HD:(hd + 1) * HD],
                                                probsT[:, pair % RING, j * KC + k, :],
                                                V[:, k, hd * HD:(hd + 1) * HD], start=False,
                                                stop=(hd == HEADS - 1 and k == KC - 1))
                last.then_inc(pv_done.sem, 1)

            pe.wait_ge(bias_ready, 3)
            pe.wait_ge(got_kv, 32)
            for k in range(KC):
                add_bias(k_psum_v[:, k, :], 1)
                product(k_psum_v[:, k, :], lambda c: ctxT[:, c, k * P:(k + 1) * P], lambda c: wkv_sb[:, c, 0:D],
                        biased=True).then_inc(k_psum, 1)
                if k == 1:
                    pe.wait_ge(idents_ready, 2)
                    turn_norm((None, 0), front, ln1, ln1_done, lnT1_psum)
            pe.wait_ge(got_wq, 16)
            queries((None, 0))
            for c in range(DC):
                nc.tensor.matmul(scores[1][:, c, :], bias3[:, 2 * D + c * P:2 * D + (c + 1) * P], ones_b[:, :],
                                 start=True, stop=False)
                product(scores[1][:, c, :], lambda i: wkv_sb[:, i, D + c * P:D + (c + 1) * P],
                        lambda i: ctxT[:, i, :], biased=True).then_inc(v_psum, 1)
            turn_queries((None, 0))
            pe.wait_ge(k_chain, 10 * (KC // 2))
            pe.wait_ge(kT_ready, 16 * KC)
            score((None, 0), 0)
            pe.wait_ge(v_chain, 2 * DC + 2)
            score((None, 0), 1)
            pe.wait_ge(V_ready, 16 * DC)
            pe.wait_ge(consts_ready, 1)

            def gate_up(t, quarter):
                if quarter == 0:
                    if number(t) == 0:
                        pe.wait_ge(w_ready, 3 * EXPERTS)
                    after(pe, y_done, shift(t, -1))
                if quarter % 2 == 0:
                    after(pe, am_done, t, quarter // 2 + 1)
                for i in range(4 * quarter, 4 * quarter + 4):
                    c, e = i // EXPERTS, i % EXPERTS
                    last = nc.tensor.matmul(ffn[:, :], am[:, c, e, :], gu_w[:, c, e, :, :].rearrange("p a n -> p (a n)"),
                                            start=(i == 0), stop=(i == DC * EXPERTS - 1))
                if quarter == 3:
                    last.then_inc(gu_psum.sem, 1)

            def down(t, c):
                after(pe, hm_done, t, c + 1)
                if c == 0:
                    after(pe, gu_done, t)
                for e in range(EXPERTS):
                    last = nc.tensor.matmul(ffn[:, 0:D], hm[:, c, e, :], dn_w[:, c, e, :],
                                            start=(c == 0 and e == 0), stop=(c == DC - 1 and e == EXPERTS - 1))
                if c == DC - 1:
                    last.then_inc(y_psum.sem, 1)

            def tile_work(t):
                ahead, back1, ffn1, ffn2 = shift(t, 1), shift(t, -1), shift(t, -2), shift(t, -3)
                for u in range(PAIRS):
                    score(t, u + 2)
                    values(t, u - LAG)
                    if u == 0 and exists(ahead):
                        after(pe, maskT_done, ffn1)
                        after(pe, qT_done, t)
                        turn_norm(ahead, front, ln1, ln1_done, lnT1_psum)
                    if u == 1 and exists(ahead):
                        queries(ahead)
                    if u == 2:
                        if exists(back1):
                            after(pe, l_chain, ffn1, 2)
                            turn_norm(back1, back, attn, attn_done, attnT_psum)
                        if exists(ffn2):
                            down(ffn2, 0)
                    if u == 3:
                        if exists(ffn2):
                            down(ffn2, 1)
                        if exists(back1):
                            after(pe, attnT_done, back1)
                            if number(back1) == 0:
                                pe.wait_ge(wp_ready, DC)
                            add_bias(back[:, 0:D], 3)
                            product(back[:, 0:D], lambda c: attnT[:, c, :], lambda c: wp_sb[:, c, :], biased=True) \
                                .then_inc(proj_psum.sem, 1)
                    if u == 4 and exists(ahead):
                        turn_queries(ahead)
                    if u in (4, 5) and exists(ffn1):
                        gate_up(ffn1, 2 * (u - 4))
                        gate_up(ffn1, 2 * (u - 4) + 1)
                    if u == 5 and exists(back1):
                        turn_norm(back1, back, ln2, ln2_done, lnT2_psum)
                    if u == 6 and exists(back1):
                        if number(back1) == 0:
                            pe.wait_ge(got_router, 16)
                        after(pe, lnT2_done, back1)
                        product(back[:, 0:EXPERTS], lambda c: lnT2[:, c, :], lambda c: rT[:, c, :]) \
                            .then_inc(logits_psum.sem, 1)
                    if u == 7 and exists(back1):
                        after(pe, mask_done, back1)
                        after(pe, qT_done, ahead)
                        for e in range(EXPERTS):
                            last = nc.tensor.transpose(front_b[:, e, :], mask[:, e:e + 1].broadcast_to([P, P]),
                                                       ident_b[:, :])
                        last.then_inc(maskT_psum.sem, 1)
                    if number(t) == 0 and u == W_FROM - 1:
                        pe.wait_ge(w_abs_ready, 3 * EXPERTS)
                        nc.tensor.matmul(ffn[:, 0:3 * EXPERTS], ones[:, :], w_abs[:, :, :].rearrange("p m e -> p (m e)"),
                                         start=True, stop=True).then_inc(w_sum_psum, 1)

            run(pe, tile_work)


def kernel(**inputs):
    import numpy as np
    import concourse.bacc as bacc
    from concourse.bass_utils import run_bass_kernel_spmd

    a = {k: np.asarray(v) for k, v in inputs.items()}
    batch, tokens, dim = a["x"].shape
    experts = a["L0_ffn_router_w"].shape[0]
    chunks = dim // 128

    def by_chunk(w):
        return w.transpose(2, 0, 1).reshape(chunks, 128, experts, -1)

    laid = {
        "x": a["x"].reshape(batch * tokens, dim),
        "ctx_t": a["ctx_2048"].reshape(-1, dim).T,
        "wq": a["L0_xattn_Wq"],
        "wkv": a["L0_xattn_Wkv"],
        "wp": a["L0_xattn_Wp"],
        "biases": np.concatenate([a["L0_xattn_bq"], a["L0_xattn_bkv"], a["L0_xattn_bp"]]).reshape(1, 4 * dim),
        "router": a["L0_ffn_router_w"].T.reshape(chunks, 128, experts),
        "w_gate_up": np.stack([by_chunk(a["L0_ffn_wg"]), by_chunk(a["L0_ffn_wu"])], axis=3),
        "w_down": by_chunk(a["L0_ffn_wd"]),
    }
    nc = bacc.Bacc("TRN2", target_bir_lowering=False, num_devices=1)
    arrays, args = {}, []
    for name, v in laid.items():
        v = np.ascontiguousarray(v)
        arrays[f"in_{name}"] = v
        args.append(nc.dram_tensor(f"in_{name}", v.shape, mybir.dt.from_np(v.dtype), kind="ExternalInput").ap())
    out = nc.dram_tensor("out_x", (batch * tokens, dim), mybir.dt.float32, kind="ExternalOutput").ap()
    cross_attention_moe(nc, *args, out)
    r = run_bass_kernel_spmd(nc, [arrays], core_ids=[0])
    return r.results[0]["out_x"].reshape(batch, tokens, dim)
```

```python
import concourse.bass as bass
from concourse import mybir
from contextlib import ExitStack
import math


class Signal:

    def __init__(self, sem, per_tile):
        self.sem, self.per_tile = sem, per_tile

    def value(self, tile, nth):
        register, offset = tile
        fixed = self.per_tile * offset + nth
        return fixed if register is None else register * self.per_tile + fixed


def cross_attention_moe(nc, x, ctx_t, wq, wkv, wp, biases, router, w_experts, out):
    fp32, bf16, fp16 = mybir.dt.float32, mybir.dt.bfloat16, mybir.dt.float16
    u8, u16, i32 = mybir.dt.uint8, mybir.dt.uint16, mybir.dt.int32
    ALU = mybir.AluOpType
    ACT = mybir.ActivationFunctionType
    AX = mybir.AxisListType

    P = 128
    TOKENS, D = x.shape
    KEYS = ctx_t.shape[1]
    EXPERTS = router.shape[2]
    HEADS = 16
    HD = D // HEADS
    DC = D // P
    KC = KEYS // P
    TILES = TOKENS // P
    PAIRS = HEADS // 2
    PARTS = 3
    BIAS_ROWS = 65
    SLOT = 64
    ROWS = PARTS * HD
    RING = 4
    LAG = 2
    ABS_SPLIT = 5
    ABS_COUNTS = (2, 2, 2, 1, 1, 1)
    WP_AT = 6
    W_FROM, W_EACH = 6, 2
    MAGIC = 1.5 * 2.0 ** 23
    LEVELS = 255.0
    OFFSET = 1024.0
    LN_EPS = 1e-5
    Q_EPS = 1e-5
    S_EPS = 1e-8

    x_v = x.rearrange("(t p) c -> t p c", p=P)
    out_v = out.rearrange("(t p) c -> t p c", p=P)

    ctx = ExitStack()
    with ctx:
        def sb(name, shape, dt):
            return ctx.enter_context(nc.sbuf_tensor(name, shape, dt))

        def pb(name, shape, dt):
            return ctx.enter_context(nc.psum_tensor(name, shape, dt))

        def sem(name):
            return ctx.enter_context(nc.semaphore(name))

        def signal(name, per_tile=1):
            return Signal(sem(name), per_tile)

        ctxT = sb("ctxT", [P, DC, KEYS], fp32)
        wq_sb = sb("wq_sb", [P, DC, D], fp32)
        wkv_sb = sb("wkv_sb", [P, DC, 2 * D], fp32)
        wp_raw = sb("wp_raw", [P, DC, D], fp32)
        wp_sb = sb("wp_sb", [P, DC, D], fp32)
        bias_row = sb("bias_row", [BIAS_ROWS, 4 * D], fp32)
        bias_r1 = sb("bias_r1", [BIAS_ROWS, 4 * D], fp32)
        bias_hi = sb("bias_hi", [BIAS_ROWS, 4 * D], bf16)
        bias_mid = sb("bias_mid", [BIAS_ROWS, 4 * D], bf16)
        bias3 = sb("bias3", [P, 4 * D], bf16)
        ones_b = sb("ones_b", [P, KEYS], bf16)
        rT = sb("rT", [P, DC, EXPERTS], fp32)
        w_raw = sb("w_raw", [P, DC, EXPERTS, 3, D], fp32)
        gu_w = sb("gu_w", [P, DC, EXPERTS, 2, D], bf16)
        dn_w = sb("dn_w", [P, DC, EXPERTS, D], bf16)
        w_abs = sb("w_abs", [P, 3, EXPERTS], fp32)
        w_scratch = sb("w_scratch", [P, DC, D], bf16)
        w_step = sb("w_step", [P, 3, EXPERTS], fp32)
        w_inv = sb("w_inv", [P, 3, EXPERTS], fp32)
        tab = sb("tab", [P, 2, EXPERTS], fp32)
        tab_t = sb("tab_t", [P, EXPERTS], fp32)
        ident = sb("ident", [P, P], fp32)
        ident_b = sb("ident_b", [P, P], bf16)
        ones = sb("ones", [P, P], fp32)
        minus_off = sb("minus_off", [P, P], fp16)
        minus_half = sb("minus_half", [P, 1], fp32)
        eps = sb("eps", [P, 1], fp32)
        minus_magic = sb("minus_magic", [P, 1], fp32)
        first_exp = sb("first_exp", [P, 1], fp32)
        ln_levels = sb("ln_levels", [P, 2], fp32)
        head_scale = sb("head_scale", [P, 2, HEADS], fp32)
        order = sb("order", [P, EXPERTS], fp32)
        kT = sb("kT", [P, PAIRS, KEYS], bf16)
        V = sb("V", [P, KC, D], fp16)

        k_max = sb("k_max", [P, KC, HEADS], fp32)
        k_step = sb("k_step", [P, KC, HEADS], fp32)
        k_inv = sb("k_inv", [P, KC, HEADS], fp32)
        k_s = sb("k_s", [P, KC, D], fp32)
        k_i = sb("k_i", [P, KC, D], fp32)
        k_q = sb("k_q", [P, KC, D], fp32)
        k_r1 = sb("k_r1", [P, KC, D], fp32)
        k_rep = sb("k_rep", [P, KC, HEADS, SLOT], bf16)
        v_max = sb("v_max", [P, DC], fp32)
        v_step = sb("v_step", [P, DC], fp32)
        v_inv = sb("v_inv", [P, DC], fp32)
        v_s = sb("v_s", [P, DC, KEYS], fp32)
        v_i = sb("v_i", [P, DC, KEYS], fp16)

        x_ln = sb("x_ln", [P, 2, D], fp32)
        x_res = sb("x_res", [P, 2, D], fp32)
        bn1 = sb("bn1", [P, 6], fp32)
        mv1 = sb("mv1", [P, 2], fp32)
        var1 = sb("var1", [P, 1], fp32)
        rstd1 = sb("rstd1", [P, 1], fp32)
        ln1 = sb("ln1", [P, D], fp32)
        lnT1 = sb("lnT1", [P, DC, P], fp32)
        q_max = sb("q_max", [P, HEADS], fp32)
        q_step = sb("q_step", [P, HEADS], fp32)
        q_inv = sb("q_inv", [P, HEADS], fp32)
        q_s = sb("q_s", [P, D], fp32)
        q_i = sb("q_i", [P, D], bf16)
        q_rep = sb("q_rep", [P, HEADS, SLOT // HD, HD], bf16)
        q_scale = sb("q_scale", [P, 2, HEADS], fp32)
        q_nscale = sb("q_nscale", [P, 2, HEADS], fp32)
        qT = sb("qT", [P, 2, PAIRS, P], bf16)
        s_max = sb("s_max", [P, 2, 2], fp32)
        nb0 = sb("nb0", [P, 2, 2], fp32)
        nb = sb("nb", [P, 2, 2], fp32)
        probs = sb("probs", [P, RING, 2, KEYS], fp16)
        probsT = sb("probsT", [P, RING, 2 * KC, P], fp16)
        z = sb("z", [P, 2, HEADS], fp32)
        rz = sb("rz", [P, HEADS], fp32)
        attn = sb("attn", [P, D], fp32)
        attnT = sb("attnT", [P, DC, P], fp32)
        x2 = sb("x2", [P, 3, D], fp32)
        bn2 = sb("bn2", [P, 6], fp32)
        mv2 = sb("mv2", [P, 2], fp32)
        var2 = sb("var2", [P, 1], fp32)
        rstd2 = sb("rstd2", [P, 1], fp32)
        ln2 = sb("ln2", [P, D], fp32)
        lnT2 = sb("lnT2", [P, DC, P], fp32)
        a_max = sb("a_max", [P, 1], fp32)
        a_step = sb("a_step", [P, 1], fp32)
        a_inv = sb("a_inv", [P, 1], fp32)
        a_m = sb("a_m", [P, D], fp32)
        a_q = sb("a_q", [P, D], bf16)
        aT = sb("aT", [P, DC, P], bf16)
        l_max = sb("l_max", [P, 1], fp32)
        l_rank = sb("l_rank", [P, EXPERTS], fp32)
        l_top = sb("l_top", [P, 1], fp32)
        mask = sb("mask", [P, EXPERTS], bf16)
        sel_t = sb("sel_t", [P, 2, EXPERTS], fp32)
        sel = sb("sel", [P, 2, 2], fp32)
        c1 = sb("c1", [P, 1], fp32)
        c2 = sb("c2", [P, 1], fp32)
        h_scale = sb("h_scale", [P, 2, 1], fp32)
        maskT = sb("maskT", [P, 2, EXPERTS, P], bf16)
        am = sb("am", [P, DC, EXPERTS, P], bf16)
        g_relu = sb("g_relu", [P, D], fp32)
        g_square = sb("g_square", [P, D], fp32)
        h = sb("h", [P, D], fp32)
        h_max = sb("h_max", [P, 1], fp32)
        h_abs = sb("h_abs", [P, 1], fp32)
        h_inv = sb("h_inv", [P, 1], fp32)
        h_mul = sb("h_mul", [P, 1], fp32)
        y_scale = sb("y_scale", [P, 1], fp32)
        h_m = sb("h_m", [P, D], fp32)
        h_q = sb("h_q", [P, D], bf16)
        hT = sb("hT", [P, DC, P], bf16)
        hm = sb("hm", [P, DC, EXPERTS, P], bf16)
        y = sb("y", [P, 2, D], fp32)

        scores = [pb(f"scores{i}", [P, 2, KEYS], fp32) for i in range(2)]
        heads_out = pb("heads_out", [P, 2 * D], fp32)
        front = pb("front", [P, 2 * D], fp32)
        back = pb("back", [P, 2 * D], fp32)
        ffn = pb("ffn", [P, 2 * D], fp32)
        front_b = front[:, :].bitcast(bf16).rearrange("p (n q) -> p n q", q=P)
        back_b = back[:, :].bitcast(bf16).rearrange("p (n q) -> p n q", q=P)
        k_psum_v = scores[0][:, :, :].rearrange("p a (b n) -> p (a b) n", n=D)

        got_bias = sem("got_bias")
        got_kv = sem("got_kv")
        got_wq = sem("got_wq")
        got_wp = sem("got_wp")
        got_router = sem("got_router")
        got_experts = [sem(f"got_experts{e}") for e in range(EXPERTS)]
        zero_ready = sem("zero_ready")
        probs_set = sem("probs_set")
        idents_ready = sem("idents_ready")
        ones_ready = sem("ones_ready")
        kv_bias_cleared = sem("kv_bias_cleared")
        qp_bias_cleared = sem("qp_bias_cleared")
        qp_bias_rest = sem("qp_bias_rest")
        kv_bias_chain = sem("kv_bias_chain")
        kv_bias_ready = sem("kv_bias_ready")
        qp_bias_chain = sem("qp_bias_chain")
        qp_bias_ready = sem("qp_bias_ready")
        k_psum = sem("k_psum")
        k_chain = [sem(f"k_chain{i}") for i in range(2)]
        k_rep_ready = sem("k_rep_ready")
        kT_psum = sem("kT_psum")
        kT_ready = sem("kT_ready")
        v_psum = sem("v_psum")
        v_chain = sem("v_chain")
        v_int_ready = sem("v_int_ready")
        V_ready = sem("V_ready")
        wp_ready = sem("wp_ready")
        reached = {e: sem(f"reached_{e}") for e in ("sp", "pool", "dve")}
        w_abs_ready = sem("w_abs_ready")
        w_abs_ready_dve = sem("w_abs_ready_dve")
        w_sum_psum = sem("w_sum_psum")
        w_step_ready = sem("w_step_ready")
        w_chain = sem("w_chain")
        w_scaled = sem("w_scaled")
        w_clipped = sem("w_clipped")
        w_ready = sem("w_ready")
        w_ready_act = sem("w_ready_act")

        x_ln_in = [sem(f"x_ln_in{i}") for i in range(2)]
        x_res_in = [sem(f"x_res_in{i}") for i in range(2)]
        y_out = [sem(f"y_out{i}") for i in range(2)]
        bn1_done = signal("bn1_done")
        mv1_done = signal("mv1_done")
        var1_done = signal("var1_done")
        rstd1_done = signal("rstd1_done")
        ln1_done = signal("ln1_done")
        lnT1_psum = signal("lnT1_psum")
        lnT1_done = signal("lnT1_done")
        q_psum = signal("q_psum")
        q_chain = signal("q_chain", 4)
        q_scale_done = signal("q_scale_done", 2)
        q_i_done = signal("q_i_done")
        q_rep_done = signal("q_rep_done")
        qT_psum = signal("qT_psum")
        qT_done = signal("qT_done")
        scores_done = signal("scores_done", PAIRS)
        max_done = signal("max_done", PAIRS)
        nb0_done = signal("nb0_done", PAIRS)
        nb_done = signal("nb_done", PAIRS)
        exp_done = signal("exp_done", HEADS)
        probsT_done = [signal(f"probsT_done{i}", 16 * PAIRS // RING) for i in range(RING)]
        pv_done = signal("pv_done", PAIRS)
        rz_done = signal("rz_done")
        attn_done = signal("attn_done")
        attnT_psum = signal("attnT_psum")
        attnT_done = signal("attnT_done")
        proj_psum = signal("proj_psum")
        x2_done = signal("x2_done")
        bn2_done = signal("bn2_done")
        mv2_done = signal("mv2_done")
        var2_done = signal("var2_done")
        rstd2_done = signal("rstd2_done")
        ln2_done = signal("ln2_done")
        lnT2_psum = signal("lnT2_psum")
        lnT2_done = signal("lnT2_done")
        logits_psum = signal("logits_psum")
        a_chain = signal("a_chain", 3)
        a_m_done = signal("a_m_done")
        a_q_done = signal("a_q_done")
        l_chain = signal("l_chain", 3)
        mask_done = signal("mask_done")
        sel_chain = signal("sel_chain")
        sel_done = signal("sel_done")
        c_chain = signal("c_chain", 2)
        h_scale_done = signal("h_scale_done")
        aT_done = signal("aT_done", 16)
        maskT_psum = signal("maskT_psum")
        maskT_done = signal("maskT_done")
        am_done = signal("am_done", DC)
        gu_psum = signal("gu_psum")
        relu_done = signal("relu_done")
        square_done = signal("square_done")
        h_done = signal("h_done")
        h_chain = signal("h_chain", 4)
        y_scale_done = signal("y_scale_done")
        h_m_done = signal("h_m_done")
        h_q_done = signal("h_q_done")
        hT_done = signal("hT_done", 16)
        last_hT_psum = sem("last_hT_psum")
        hm_done = signal("hm_done", DC)
        y_psum = signal("y_psum")
        y_done = signal("y_done")

        KV, QP = slice(0, 2 * D), slice(2 * D, 4 * D)

        key_banks = [a[:, :].bitcast(bf16).rearrange("p (n q) -> p n q", q=P) for a in (back, ffn, heads_out, back)]

        def shift(tile, by):
            return tile[0], tile[1] + by

        def number(tile):
            return tile[1] if tile[0] is None else None

        def exists(tile):
            return tile[0] is not None or 0 <= tile[1] < TILES

        def unit(tile, pair):
            return shift(tile, pair // PAIRS), pair % PAIRS

        def after(eng, what, tile, nth=None):
            if not exists(tile):
                return
            eng.wait_ge(what.sem, what.value(tile, what.per_tile if nth is None else nth))

        def parity(tile):
            return tile[1] % 2

        LOOP_FROM, LOOP_TO = 4, TILES - 2

        def run(eng, body):
            for t in range(LOOP_FROM):
                body((None, t))
            with eng.Fori(0, (LOOP_TO - LOOP_FROM) // 2) as turn:
                body((turn * 2, LOOP_FROM))
                body((turn * 2, LOOP_FROM + 1))
            for t in range(LOOP_TO, TILES):
                body((None, t))

        block = ctx.enter_context(nc.Block())

        def carry(eng, name):
            eng.sem_inc(reached[name], 1)

        THIRD_LAST, NEXT_LAST, LAST = (None, TILES - 3), (None, TILES - 2), (None, TILES - 1)

        def gate_bank(t):
            if number(t) in (TILES - 2, TILES - 1):
                return scores[0][:, parity(t), :]
            return ffn[:, :]

        def mask_bank(t):
            return front_b if number(t) in (TILES - 2, TILES - 1) else back_b

        def x2_slot(t):
            return 2 if number(t) == TILES - 1 else parity(t)

        def arrived(eng, sems, t):
            p = parity(t)
            fixed = 8 * (t[1] - p) + 16
            eng.wait_ge(sems[p], fixed if t[0] is None else t[0] * 8 + fixed)

        def by_head(a):
            return a.rearrange("p (h d) -> p h d", d=HD)

        @block.sync
        def _(sp):
            def rows(v, t):
                return v[t[1]] if t[0] is None else v[t[0] + t[1]]

            def load(into, done, t):
                sp.dma_start(into[:, parity(t), :], rows(x_v, t)).then_inc(done[parity(t)], 16)

            sp.dma_start(bias_row[:, :], biases.broadcast_to([BIAS_ROWS, 4 * D])).then_inc(got_bias, 16)
            load(x_ln, x_ln_in, (None, 0))
            sp.dma_start(wkv_sb[:, :, :], wkv.rearrange("(c p) n -> p c n", p=P)).then_inc(got_kv, 16)
            load(x_ln, x_ln_in, (None, 1))
            sp.dma_start(wp_raw[:, :, :], wp.rearrange("(c p) n -> p c n", p=P)).then_inc(got_wp, 16)
            sp.dma_start(rT[:, :, :], router.rearrange("c p e -> p c e")).then_inc(got_router, 16)
            load(x_res, x_res_in, (None, 0))
            load(x_res, x_res_in, (None, 1))
            for c in range(DC):
                sp.wait_ge(v_int_ready, c + 1)
                sp.dma_start_transpose(V[:, :, c * P:(c + 1) * P], v_i[:, c, :]).then_inc(V_ready, 16)

            def sp_after(what, tile, nth=None):
                if exists(tile):
                    after(sp, what, tile, nth)
                    carry(sp, "sp")

            def turn_probs(t, pair):
                sp_after(exp_done, t, 2 * pair + 2)
                before, b_pair = unit(t, pair - RING)
                sp_after(pv_done, before, b_pair + 1)
                sp.dma_start_transpose(probsT[:, pair % RING, :, :],
                                       probs[:, pair % RING, :, :].rearrange("p a k -> p (a k)")) \
                    .then_inc(probsT_done[pair % RING].sem, 16)

            def store(t):
                sp_after(y_done, t)
                sp.dma_start(rows(out_v, t), y[:, parity(t), :]).then_inc(y_out[parity(t)], 16)

            def turn_input(t):
                sp_after(a_q_done, t)
                sp_after(am_done, shift(t, -1))
                sp.dma_start_transpose(aT[:, :, :], a_q[:, :]).then_inc(aT_done.sem, 16)

            def turn_hidden(t):
                sp_after(h_q_done, t)
                sp_after(hm_done, shift(t, -1))
                sp.dma_start_transpose(hT[:, :, :], h_q[:, :]).then_inc(hT_done.sem, 16)

            def tile_work(t):
                ahead, ahead2 = shift(t, 1), shift(t, 2)
                back1, ffn1, ffn2 = shift(t, -1), shift(t, -2), shift(t, -3)
                for u in range(PAIRS):
                    if exists(t):
                        turn_probs(t, u)
                    if u == 0 and exists(ahead2):
                        sp_after(ln1_done, t)
                        load(x_ln, x_ln_in, ahead2)
                    if u == 1 and exists(ffn2):
                        turn_hidden(ffn2)
                    if u == 6 and exists(ahead) and number(t) != 0:
                        sp_after(x2_done, back1)
                        load(x_res, x_res_in, ahead)
                    if u == 6 and exists(ffn2):
                        store(ffn2)
                    if u == 7 and exists(back1):
                        turn_input(back1)

            run(sp, tile_work)
            turn_hidden(THIRD_LAST)
            store(THIRD_LAST)
            turn_input(LAST)
            turn_hidden(NEXT_LAST)
            store(NEXT_LAST)
            store(LAST)
            for i in range(2):
                sp.wait_ge(y_out[i], 16 * (TILES // 2 + 1))

        def raw(n):
            return w_raw[:, :, n // 3, n % 3, :]

        def made(n):
            m, e = n % 3, n // 3
            return gu_w[:, :, e, m, :] if m < 2 else dn_w[:, :, e, :]

        @block.scalar
        def _(act):
            act.dma_start(ctxT[:, :, :], ctx_t.rearrange("(c p) k -> p c k", p=P)).then_inc(got_kv, 16)
            act.dma_start(wq_sb[:, :, :], wq.rearrange("(c p) n -> p c n", p=P)).then_inc(got_wq, 16)
            act.wait_ge(zero_ready, 1)
            nc.scalar.activation(first_exp[:, :], eps[:, :], ACT.Exp)
            act.wait_ge(got_kv, 32)
            for e in range(EXPERTS):
                act.dma_start(w_raw[:, :, e, :, :], w_experts[:, :, e].rearrange("c p m n -> p c m n")) \
                    .then_inc(got_experts[e], 16)

            def weights_abs(e):
                act.wait_ge(got_experts[e], 16)
                for m in range(3):
                    if 3 * e + m:
                        act.wait_ge(w_abs_ready, 3 * e + m)
                    nc.scalar.activation(w_scratch[:, :, :], raw(3 * e + m), ACT.Abs,
                                         accum_out=w_abs[:, m, e:e + 1]).then_inc(w_abs_ready, 1)

            def from_psum(psum_ready, done, t, to, bank, func=ACT.Copy):
                after(act, psum_ready, t)
                nc.scalar.activation(to, bank, func).then_inc(done.sem, 1)

            def chunks(bank):
                return bank[:, 0:D].rearrange("p (c q) -> p c q", q=P)

            def first_norm_out(t):
                from_psum(lnT1_psum, lnT1_done, t, lnT1[:, :, :], chunks(front))

            def queries_out(t):
                after(act, scores_done, shift(t, -2))
                from_psum(qT_psum, qT_done, t, qT[:, parity(t), :, :], front_b)

            def attention_out(t):
                from_psum(attnT_psum, attnT_done, t, attnT[:, :, :], chunks(back))

            def second_norm_out(t):
                from_psum(lnT2_psum, lnT2_done, t, lnT2[:, :, :], chunks(back))

            def mask_out(t):
                after(act, hm_done, shift(t, -2))
                from_psum(maskT_psum, maskT_done, t, maskT[:, parity(t), :, :], mask_bank(t))

            def gate_out(t):
                from_psum(gu_psum, relu_done, t, g_relu[:, :], gate_bank(t)[:, 0:D], ACT.Relu)
                after(act, relu_done, t)
                after(act, h_done, shift(t, -1))
                nc.scalar.activation(g_square[:, :], g_relu[:, :], ACT.Square).then_inc(square_done.sem, 1)

            def exps(t, pair):
                t, pair = unit(t, pair)
                if not exists(t):
                    return
                after(act, nb_done, t, pair + 1)
                before, b_pair = unit(t, pair - RING)
                after(act, probsT_done[b_pair % RING], before, 16 * (b_pair // RING + 1))
                if pair == 0:
                    after(act, rz_done, shift(t, -2))
                i, s = pair % 2, pair % RING
                low = probs[:, s, :, :].rearrange("p a b -> p (a b)").bitcast(u8) \
                    .rearrange("p (a b two) -> p a b two", a=2, two=2)
                for j in range(2):
                    hd = 2 * pair + j
                    nc.scalar.activation(low[:, j, :, 0], scores[i][:, j, :], ACT.Exp,
                                         bias=nb[:, i, j:j + 1], scale=q_scale[:, parity(t), hd:hd + 1],
                                         accum_out=z[:, parity(t), hd:hd + 1]).then_inc(exp_done.sem, 1)

            def weights_ternary(n):
                for i in range(n + 1, n + W_EACH, 2):
                    act.wait_ge(w_scaled, i + 1)
                    nc.scalar.activation(made(i), raw(i), ACT.Sign, bias=minus_magic[:, :]).then_inc(w_ready_act, 1)

            first_norm_out((None, 0))
            act.wait_ge(qp_bias_cleared, 1)
            act.wait_ge(got_bias, 16)
            nc.scalar.activation(bias_hi[:, QP], bias_row[:, QP], ACT.Copy).then_inc(qp_bias_chain, 1)
            act.wait_ge(qp_bias_chain, 1)
            nc.scalar.activation(bias3[0:1, QP], bias_hi[0:1, QP], ACT.Copy).then_inc(qp_bias_ready, 1)
            weights_abs(0)
            act.wait_ge(qp_bias_rest, 1)
            nc.scalar.activation(bias_mid[:, QP], bias_r1[:, QP], ACT.Copy).then_inc(qp_bias_chain, 1)
            act.wait_ge(qp_bias_chain, 2)
            nc.scalar.activation(bias3[32:33, QP], bias_mid[32:33, QP], ACT.Copy).then_inc(qp_bias_ready, 1)
            weights_abs(1)
            act.wait_ge(qp_bias_rest, 2)
            nc.scalar.activation(bias3[64:65, QP], bias_row[64:65, QP], ACT.Copy).then_inc(qp_bias_ready, 1)
            weights_abs(2)
            for k in range(KC):
                act.wait_ge(kT_psum, k + 1)
                nc.scalar.activation(kT[:, :, k * P:(k + 1) * P], key_banks[k], ACT.Copy).then_inc(kT_ready, 1)
                if k == 1:
                    weights_abs(3)
            queries_out((None, 0))
            for e in range(4, ABS_SPLIT):
                weights_abs(e)
            act.wait_ge(probs_set, RING // 2)
            exps((None, 0), 0)
            first_norm_out((None, 1))

            def tile_work(t):
                ahead, ahead2 = shift(t, 1), shift(t, 2)
                back1, ffn1, ffn2 = shift(t, -1), shift(t, -2), shift(t, -3)
                for u in range(PAIRS):
                    exps(t, u + 1)
                    if t[0] is None and 0 <= 8 * t[1] + u - W_FROM - 1 < 3 * EXPERTS // W_EACH:
                        weights_ternary(W_EACH * (8 * t[1] + u - W_FROM - 1))
                    if u == 0:
                        if exists(ffn1):
                            mask_out(ffn1)
                    if u == 2:
                        if exists(back1):
                            attention_out(back1)
                    if u == 4:
                        if exists(ahead):
                            queries_out(ahead)
                    if u == 6:
                        if exists(ffn1):
                            gate_out(ffn1)
                        if exists(back1):
                            second_norm_out(back1)
                    if u == 7:
                        if exists(ahead2):
                            first_norm_out(ahead2)

            run(act, tile_work)
            attention_out(LAST)
            mask_out(NEXT_LAST)
            second_norm_out(LAST)
            gate_out(NEXT_LAST)
            mask_out(LAST)
            gate_out(LAST)
            after(act, hm_done, NEXT_LAST)
            act.wait_ge(last_hT_psum, 1)
            nc.scalar.activation(hT[:, :, :], front_b[:, 0:DC, :], ACT.Copy).then_inc(hT_done.sem, 16)

        @block.gpsimd
        def _(pool):
            pool.wait_ge(zero_ready, 1)
            nc.gpsimd.affine_select(out=ident[:, :], in_=ident[:, :], compare_op=ALU.not_equal, fill=1.0,
                                    base=0, pattern=[[-1, P]], channel_multiplier=1).then_inc(idents_ready, 1)
            nc.gpsimd.memset(bias3[:, QP].bitcast(fp32), 0.0).then_inc(qp_bias_cleared, 1)
            nc.gpsimd.memset(ones_b[:, :], 1.0).then_inc(ones_ready, 1)
            nc.gpsimd.memset(k_rep[:, :, :, ROWS:SLOT].rearrange("p k h s -> p (k h) s"), 0.0).then_inc(ones_ready, 1)

            def rstd(t, mv, mv_done, var, v_done, r, done):
                after(pool, mv_done, t)
                nc.gpsimd.tensor_tensor(var[:, :], mv[:, 1:2], eps[:, :], ALU.add).then_inc(v_done.sem, 1)
                after(pool, v_done, t)
                nc.gpsimd.tensor_tensor(r[:, :], var[:, :], minus_half[:, :], ALU.pow).then_inc(done.sem, 1)

            def rounded(t, x, x_ready, nth, inverse, m, m_done, q, q_read, q_done):
                after(pool, x_ready, t, nth)
                carry(pool, "pool")
                nc.gpsimd.tensor_scalar(m[:, :], x[:, :], inverse[:, :], MAGIC, ALU.mult, ALU.add) \
                    .then_inc(m_done.sem, 1)
                after(pool, m_done, t)
                after(pool, q_read, shift(t, -1))
                carry(pool, "pool")
                nc.gpsimd.tensor_scalar(q[:, :], m[:, :], -MAGIC, 1.0, ALU.add, ALU.mult).then_inc(q_done.sem, 1)

            def first_rstd(t):
                rstd(t, mv1, mv1_done, var1, var1_done, rstd1, rstd1_done)

            def second_rstd(t):
                rstd(t, mv2, mv2_done, var2, var2_done, rstd2, rstd2_done)

            def bias(t, pair):
                t, pair = unit(t, pair)
                if not exists(t):
                    return
                i = pair % 2
                after(pool, max_done, t, pair + 1)
                if pair == 0:
                    after(pool, q_scale_done, t)
                before, b_pair = unit(t, pair - 2)
                after(pool, exp_done, before, 2 * b_pair + 2)
                nc.gpsimd.tensor_tensor(nb0[:, i, :], s_max[:, i, :],
                                        q_nscale[:, parity(t), 2 * pair:2 * pair + 2], ALU.mult) \
                    .then_inc(nb0_done.sem, 1)
                after(pool, nb0_done, t, pair + 1)
                nc.gpsimd.tensor_tensor(nb[:, i, :], nb0[:, i, :], ln_levels[:, :], ALU.add) \
                    .then_inc(nb_done.sem, 1)

            def q_scales(t):
                after(pool, q_chain, t, 2)
                after(pool, exp_done, shift(t, -2))
                for i, scaled in enumerate((q_nscale, q_scale)):
                    nc.gpsimd.tensor_tensor(scaled[:, parity(t), :], q_step[:, :], head_scale[:, i, :],
                                            ALU.mult).then_inc(q_scale_done.sem, 1)

            first_rstd((None, 0))
            for i in range(RING // 2):
                nc.gpsimd.memset(probs[:, 2 * i:2 * i + 2, :, :], OFFSET).then_inc(probs_set, 1)
            first_rstd((None, 1))
            pool.wait_ge(qp_bias_chain, 1)
            nc.gpsimd.tensor_tensor(bias_r1[:, QP], bias_row[:, QP], bias_hi[:, QP], ALU.subtract) \
                .then_inc(qp_bias_rest, 1)
            pool.wait_ge(qp_bias_chain, 2)
            pool.wait_ge(qp_bias_rest, 1)
            nc.gpsimd.tensor_tensor(bias_row[:, QP], bias_r1[:, QP], bias_mid[:, QP], ALU.subtract) \
                .then_inc(qp_bias_rest, 1)
            for i in range(2):
                nc.gpsimd.memset(y[:, i, :], 0.0).then_inc(y_out[i], 16)
            q_scales((None, 0))
            bias((None, 0), 0)
            bias((None, 0), 1)

            def input_rounded(t):
                rounded(t, ln2, a_chain, 3, a_inv, a_m, a_m_done, a_q, aT_done, a_q_done)

            def input_square(t):
                after(pool, a_chain, t, 2)
                nc.gpsimd.tensor_tensor(c1[:, :], a_step[:, :], a_step[:, :], ALU.mult).then_inc(c_chain.sem, 1)

            def hidden_scale(t):
                after(pool, sel_done, t)
                nc.gpsimd.tensor_tensor(c2[:, :], a_step[:, :], sel[:, parity(t), 0:1], ALU.mult) \
                    .then_inc(c_chain.sem, 1)
                after(pool, c_chain, t)
                nc.gpsimd.tensor_tensor(h_scale[:, parity(t), :], c1[:, :], c2[:, :], ALU.mult) \
                    .then_inc(h_scale_done.sem, 1)

            def hidden_rounded(t):
                rounded(t, h, h_chain, 4, h_mul, h_m, h_m_done, h_q, hT_done, h_q_done)

            def result_scale(t):
                after(pool, y_done, shift(t, -1))
                nc.gpsimd.tensor_tensor(y_scale[:, :], h_abs[:, :], sel[:, parity(t), 1:2], ALU.mult) \
                    .then_inc(y_scale_done.sem, 1)

            def weights_scaled(n):
                m, e = n % 3, n // 3
                pool.wait_ge(w_step_ready, 2)
                nc.gpsimd.tensor_scalar(raw(n), raw(n), w_inv[:, m, e:e + 1], MAGIC, ALU.mult, ALU.add) \
                    .then_inc(w_scaled, 1)

            def tile_work(t):
                ahead, ahead2 = shift(t, 1), shift(t, 2)
                back1, ffn1, ffn2 = shift(t, -1), shift(t, -2), shift(t, -3)
                for u in range(PAIRS):
                    bias(t, u + 2)
                    if t[0] is None and 0 <= 8 * t[1] + u - W_FROM < 3 * EXPERTS // W_EACH:
                        for n in range(W_EACH):
                            weights_scaled(W_EACH * (8 * t[1] + u - W_FROM) + n)
                    if u == 0:
                        if exists(ffn2):
                            hidden_rounded(ffn2)
                    if u == 1:
                        if exists(ffn2):
                            result_scale(ffn2)
                    if u == 2:
                        if exists(ahead):
                            q_scales(ahead)
                    if u == 4:
                        if exists(ahead2):
                            first_rstd(ahead2)
                        if exists(ffn1):
                            hidden_scale(ffn1)
                        if exists(back1):
                            second_rstd(back1)
                    if u == 6:
                        if exists(back1):
                            input_rounded(back1)
                    if u == 7:
                        if exists(back1):
                            input_square(back1)

            run(pool, tile_work)
            hidden_rounded(THIRD_LAST)
            result_scale(THIRD_LAST)
            hidden_scale(NEXT_LAST)
            second_rstd(LAST)
            input_rounded(LAST)
            input_square(LAST)
            hidden_rounded(NEXT_LAST)
            result_scale(NEXT_LAST)
            hidden_scale(LAST)
            hidden_rounded(LAST)
            result_scale(LAST)

        @block.vector
        def _(dve):
            nc.vector.memset(ident[:, :], 0.0)
            nc.vector.memset(minus_half[:, :], -0.5)
            nc.vector.memset(eps[:, :], LN_EPS)
            nc.vector.memset(minus_magic[:, :], -MAGIC)
            nc.vector.memset(ln_levels[:, :], math.log(LEVELS))
            nc.vector.memset(head_scale[:, 0, :], -1.0 / math.sqrt(HD))
            nc.vector.memset(head_scale[:, 1, :], 1.0 / math.sqrt(HD)).then_inc(zero_ready, 1)
            nc.vector.memset(bias3[:, KV].bitcast(fp32), 0.0).then_inc(kv_bias_cleared, 1)
            dve.wait_ge(kv_bias_cleared, 1)
            dve.wait_ge(got_bias, 16)
            nc.vector.tensor_copy(bias_hi[:, KV], bias_row[:, KV]).then_inc(kv_bias_chain, 1)
            dve.wait_ge(kv_bias_chain, 1)
            nc.vector.tensor_copy(bias3[0:1, KV], bias_hi[0:1, KV]).then_inc(kv_bias_ready, 1)
            nc.vector.tensor_tensor(bias_r1[:, KV], bias_row[:, KV], bias_hi[:, KV], ALU.subtract) \
                .then_inc(kv_bias_chain, 1)
            dve.wait_ge(kv_bias_chain, 2)
            nc.vector.tensor_copy(bias_mid[:, KV], bias_r1[:, KV]).then_inc(kv_bias_chain, 1)
            dve.wait_ge(kv_bias_chain, 3)
            nc.vector.tensor_copy(bias3[32:33, KV], bias_mid[32:33, KV]).then_inc(kv_bias_ready, 1)
            nc.vector.tensor_tensor(bias_row[:, KV], bias_r1[:, KV], bias_mid[:, KV], ALU.subtract) \
                .then_inc(kv_bias_chain, 1)
            dve.wait_ge(kv_bias_chain, 4)
            nc.vector.tensor_copy(bias3[64:65, KV], bias_row[64:65, KV]).then_inc(kv_bias_ready, 1)

            def first_stats(t):
                arrived(dve, x_ln_in, t)
                nc.vector.bn_stats(bn1[:, :], x_ln[:, parity(t), :]).then_inc(bn1_done.sem, 1)

            def first_aggregate(t):
                after(dve, bn1_done, t)
                carry(dve, "dve")
                nc.vector.bn_aggr(mv1[:, :], bn1[:, :]).then_inc(mv1_done.sem, 1)

            def first_norm(t):
                after(dve, rstd1_done, t)
                after(dve, lnT1_psum, shift(t, -1))
                nc.vector.tensor_scalar(ln1[:, :], x_ln[:, parity(t), :], mv1[:, 0:1], rstd1[:, :],
                                        ALU.subtract, ALU.mult).then_inc(ln1_done.sem, 1)

            def query_steps(t):
                after(dve, q_psum, t)
                nc.vector.tensor_reduce(q_max[:, :], by_head(front[:, 0:D]), axis=AX.X,
                                        op=ALU.max, apply_absolute_value=True).then_inc(q_chain.sem, 1)
                after(dve, q_chain, t, 1)
                after(dve, q_scale_done, shift(t, -1))
                nc.vector.tensor_scalar(q_step[:, :], q_max[:, :], 1.0 / 127.0, S_EPS * math.sqrt(HD),
                                        ALU.mult, ALU.max).then_inc(q_chain.sem, 1)

            def query_inverse(t):
                after(dve, q_chain, t, 2)
                nc.vector.reciprocal(q_inv[:, :], q_step[:, :]).then_inc(q_chain.sem, 1)

            def query_scaled(t):
                after(dve, q_chain, t, 3)
                nc.vector.tensor_tensor(by_head(q_s[:, :]), by_head(front[:, 0:D]),
                                        q_inv[:, :].unsqueeze(2).broadcast_to([P, HEADS, HD]),
                                        ALU.mult).then_inc(q_chain.sem, 1)

            def query_rounded(t):
                after(dve, q_chain, t, 4)
                after(dve, q_rep_done, shift(t, -1))
                nc.vector.tensor_scalar(q_i[:, :], q_s[:, :], MAGIC, MAGIC, ALU.add, ALU.subtract) \
                    .then_inc(q_i_done.sem, 1)

            def query_copies(t):
                after(dve, q_i_done, t)
                after(dve, qT_psum, shift(t, -1))
                nc.vector.tensor_copy(q_rep[:, :, :, :],
                                      by_head(q_i[:, :]).unsqueeze(2).broadcast_to([P, HEADS, SLOT // HD, HD])) \
                    .then_inc(q_rep_done.sem, 1)

            def maxima(t, pair):
                t, pair = unit(t, pair)
                if not exists(t):
                    return
                after(dve, scores_done, t, pair + 1)
                nc.vector.tensor_reduce(s_max[:, pair % 2, :], scores[pair % 2][:, :, :], axis=AX.X, op=ALU.max) \
                    .then_inc(max_done.sem, 1)

            first_stats((None, 0))
            first_aggregate((None, 0))
            nc.vector.memset(ones[:, :], 1.0)
            nc.vector.memset(minus_off[:, :], -OFFSET)
            for e in range(EXPERTS):
                nc.vector.memset(order[:, e:e + 1], float(EXPERTS - e))
            dve.wait_ge(idents_ready, 1)
            nc.vector.tensor_copy(ident_b[:, :], ident[:, :]).then_inc(idents_ready, 1)
            first_norm((None, 0))
            first_stats((None, 1))
            first_aggregate((None, 1))

            def half(i):
                return slice(i * KC // 2, (i + 1) * KC // 2)

            def heads_of(a, i):
                return a[:, half(i), :].rearrange("p k (h d) -> p (k h) d", d=HD)

            def flat(a, i):
                return a[:, half(i), :].rearrange("p k h -> p (k h)")

            def spread(a, i):
                return flat(a, i).unsqueeze(2).broadcast_to([P, KC // 2 * HEADS, HD])

            def part(j, i):
                return k_rep[:, half(i), :, j * HD:(j + 1) * HD].rearrange("p k h d -> p (k h) d")

            def key_max(i):
                dve.wait_ge(k_psum, (i + 1) * KC // 2)
                nc.vector.tensor_reduce(flat(k_max, i), heads_of(k_psum_v, i), axis=AX.X, op=ALU.max,
                                        apply_absolute_value=True).then_inc(k_chain[i], 1)

            def key_step(i):
                dve.wait_ge(k_chain[i], 1)
                nc.vector.tensor_scalar(flat(k_step, i), flat(k_max, i), 1.0 / 127.0, S_EPS, ALU.mult, ALU.max) \
                    .then_inc(k_chain[i], 1)

            def key_inverse(i):
                dve.wait_ge(k_chain[i], 2)
                nc.vector.reciprocal(flat(k_inv, i), flat(k_step, i)).then_inc(k_chain[i], 1)

            def key_scaled(i):
                dve.wait_ge(k_chain[i], 3)
                nc.vector.tensor_tensor(heads_of(k_s, i), heads_of(k_psum_v, i), spread(k_inv, i), ALU.mult) \
                    .then_inc(k_chain[i], 1)

            def key_rounded(i):
                dve.wait_ge(k_chain[i], 4)
                nc.vector.tensor_scalar(k_i[:, half(i), :], k_s[:, half(i), :], MAGIC, MAGIC,
                                        ALU.add, ALU.subtract).then_inc(k_chain[i], 1)

            def key_value(i):
                dve.wait_ge(k_chain[i], 5)
                nc.vector.tensor_tensor(heads_of(k_q, i), heads_of(k_i, i), spread(k_step, i), ALU.mult) \
                    .then_inc(k_chain[i], 1)

            def key_part_0(i):
                dve.wait_ge(k_chain[i], 6)
                nc.vector.tensor_copy(part(0, i), heads_of(k_q, i)).then_inc(k_chain[i], 1)

            def key_rest_0(i):
                dve.wait_ge(k_chain[i], 7)
                nc.vector.tensor_tensor(heads_of(k_r1, i), heads_of(k_q, i), part(0, i), ALU.subtract) \
                    .then_inc(k_chain[i], 1)

            def key_part_1(i):
                dve.wait_ge(k_chain[i], 8)
                nc.vector.tensor_copy(part(1, i), heads_of(k_r1, i)).then_inc(k_chain[i], 1)

            def key_rest_1(i):
                dve.wait_ge(k_chain[i], 9)
                nc.vector.tensor_tensor(heads_of(k_s, i), heads_of(k_r1, i), part(1, i), ALU.subtract) \
                    .then_inc(k_chain[i], 1)

            def key_part_2(i):
                dve.wait_ge(k_chain[i], 10)
                if i == 0:
                    dve.wait_ge(ones_ready, 2)
                nc.vector.tensor_copy(part(2, i), heads_of(k_s, i)).then_inc(k_rep_ready, 1)

            key_max(0)
            key_step(0)
            key_inverse(0)
            key_scaled(0)
            key_max(1)
            key_rounded(0)
            key_step(1)
            key_value(0)
            key_inverse(1)
            key_part_0(0)
            key_scaled(1)
            key_rest_0(0)
            key_rounded(1)
            key_part_1(0)
            key_value(1)
            key_rest_1(0)
            key_part_0(1)
            key_part_2(0)
            key_rest_0(1)
            query_steps((None, 0))
            key_part_1(1)
            query_inverse((None, 0))
            key_rest_1(1)
            query_scaled((None, 0))
            key_part_2(1)
            query_rounded((None, 0))
            first_norm((None, 1))
            query_copies((None, 0))

            for c in range(DC):
                dve.wait_ge(v_psum, c + 1)
                nc.vector.tensor_reduce(v_max[:, c:c + 1], scores[1][:, c, :], axis=AX.X, op=ALU.max,
                                        apply_absolute_value=True).then_inc(v_chain, 1)
            dve.wait_ge(v_chain, DC)
            nc.vector.tensor_scalar(v_step[:, :], v_max[:, :], 1.0 / 127.0, S_EPS, ALU.mult, ALU.max) \
                .then_inc(v_chain, 1)
            dve.wait_ge(v_chain, DC + 1)
            nc.vector.reciprocal(v_inv[:, :], v_step[:, :]).then_inc(v_chain, 1)
            dve.wait_ge(v_chain, DC + 2)
            for c in range(DC):
                nc.vector.tensor_scalar(v_s[:, c, :], scores[1][:, c, :], v_inv[:, c:c + 1], MAGIC,
                                        ALU.mult, ALU.add).then_inc(v_chain, 1)
            for c in range(DC):
                dve.wait_ge(v_chain, DC + 3 + c)
                nc.vector.tensor_scalar(v_i[:, c, :], v_s[:, c, :], MAGIC, 0.0, ALU.subtract, ALU.add) \
                    .then_inc(v_int_ready, 1)
            maxima((None, 0), 0)
            maxima((None, 0), 1)
            def output_rows():
                dve.wait_ge(got_wp, 16)
                for c in range(DC):
                    nc.vector.tensor_scalar(wp_sb[:, c, :], wp_raw[:, c, :], v_step[:, c:c + 1], 0.0,
                                            ALU.mult, ALU.add).then_inc(wp_ready, 1)

            def weights_abs(n):
                m, e = n % 3, n // 3
                dve.wait_ge(got_experts[e], 16)
                nc.vector.tensor_reduce(w_abs[:, m, e:e + 1], raw(n), axis=AX.XY, op=ALU.add,
                                        apply_absolute_value=True).then_inc(w_abs_ready_dve, 1)

            for n in range(3 * ABS_SPLIT, 3 * ABS_SPLIT + ABS_COUNTS[0]):
                weights_abs(n)

            def weight_steps():
                dve.wait_ge(w_sum_psum, 1)
                nc.vector.tensor_scalar(w_step[:, :, :].rearrange("p m e -> p (m e)"), ffn[:, 0:3 * EXPERTS],
                                        1.0 / (D * D), Q_EPS, ALU.mult, ALU.max).then_inc(w_step_ready, 1)
                dve.wait_ge(w_step_ready, 1)
                nc.vector.reciprocal(w_inv[:, :, :], w_step[:, :, :]).then_inc(w_step_ready, 1)
                nc.vector.tensor_tensor(tab_t[:, :], w_step[:, 0, :], w_step[:, 0, :], ALU.mult).then_inc(w_chain, 1)
                nc.vector.tensor_scalar(tab[:, 1, :], w_step[:, 2, :], 1.0 / 127.0, 0.0, ALU.mult, ALU.add) \
                    .then_inc(w_chain, 1)
                dve.wait_ge(w_chain, 2)
                nc.vector.tensor_tensor(tab[:, 0, :], tab_t[:, :], w_step[:, 1, :], ALU.mult).then_inc(w_chain, 1)

            def weights_ternary(n):
                for i in range(n, n + W_EACH, 2):
                    dve.wait_ge(w_scaled, i + 1)
                    nc.vector.tensor_scalar(made(i), raw(i), MAGIC, 1.0, ALU.subtract, ALU.min) \
                        .then_inc(w_clipped, 1)
                for i in range(n, n + W_EACH, 2):
                    dve.wait_ge(w_clipped, i // 2 + 1)
                    nc.vector.tensor_scalar(made(i), made(i), -1.0, 1.0, ALU.max, ALU.mult).then_inc(w_ready, 1)

            def sums_inverse(t):
                after(dve, exp_done, t)
                after(dve, attn_done, shift(t, -1))
                nc.vector.reciprocal(rz[:, :], z[:, parity(t), :]).then_inc(rz_done.sem, 1)

            def heads_normalised(t):
                after(dve, rz_done, t)
                after(dve, pv_done, t)
                after(dve, attnT_psum, shift(t, -1))
                nc.vector.tensor_tensor(by_head(attn[:, :]), by_head(heads_out[:, 0:D]),
                                        rz[:, :].unsqueeze(2).broadcast_to([P, HEADS, HD]), ALU.mult) \
                    .then_inc(attn_done.sem, 1)

            def residual(t):
                arrived(dve, x_res_in, t)
                after(dve, proj_psum, t)
                if number(t) != TILES - 1:
                    after(dve, y_done, shift(t, -2))
                nc.vector.tensor_tensor(x2[:, x2_slot(t), :], back[:, 0:D], x_res[:, parity(t), :], ALU.add) \
                    .then_inc(x2_done.sem, 1)

            def second_stats(t):
                after(dve, x2_done, t)
                nc.vector.bn_stats(bn2[:, :], x2[:, x2_slot(t), :]).then_inc(bn2_done.sem, 1)

            def second_aggregate(t):
                after(dve, bn2_done, t)
                carry(dve, "dve")
                nc.vector.bn_aggr(mv2[:, :], bn2[:, :]).then_inc(mv2_done.sem, 1)

            def second_norm(t):
                after(dve, rstd2_done, t)
                after(dve, lnT2_psum, shift(t, -1))
                nc.vector.tensor_scalar(ln2[:, :], x2[:, x2_slot(t), :], mv2[:, 0:1], rstd2[:, :],
                                        ALU.subtract, ALU.mult).then_inc(ln2_done.sem, 1)

            def input_max(t):
                after(dve, ln2_done, t)
                nc.vector.tensor_reduce(a_max[:, :], ln2[:, :], axis=AX.X, op=ALU.max,
                                        apply_absolute_value=True).then_inc(a_chain.sem, 1)

            def input_step(t):
                after(dve, a_chain, t, 1)
                after(dve, h_scale_done, shift(t, -1))
                nc.vector.tensor_scalar(a_step[:, :], a_max[:, :], 1.0 / 127.0, Q_EPS / 127.0,
                                        ALU.mult, ALU.max).then_inc(a_chain.sem, 1)

            def input_inverse(t):
                after(dve, a_chain, t, 2)
                nc.vector.reciprocal(a_inv[:, :], a_step[:, :]).then_inc(a_chain.sem, 1)

            def logit_max(t):
                after(dve, logits_psum, t)
                nc.vector.tensor_reduce(l_max[:, :], back[:, 0:EXPERTS], axis=AX.X, op=ALU.max) \
                    .then_inc(l_chain.sem, 1)

            def logit_rank(t):
                after(dve, l_chain, t, 1)
                nc.vector.scalar_tensor_tensor(out=l_rank[:, :], in0=back[:, 0:EXPERTS], scalar=l_max[:, :],
                                               in1=order[:, :], op0=ALU.is_equal, op1=ALU.mult) \
                    .then_inc(l_chain.sem, 1)

            def logit_top(t):
                after(dve, l_chain, t, 2)
                nc.vector.tensor_reduce(l_top[:, :], l_rank[:, :], axis=AX.X, op=ALU.max).then_inc(l_chain.sem, 1)

            def expert_mask(t):
                after(dve, l_chain, t, 3)
                after(dve, maskT_psum, shift(t, -1))
                nc.vector.tensor_scalar(mask[:, :], l_rank[:, :], l_top[:, :], 1.0, ALU.is_equal, ALU.mult) \
                    .then_inc(mask_done.sem, 1)

            def expert_steps(t):
                after(dve, mask_done, t)
                nc.vector.tensor_tensor(sel_t[:, :, :], mask[:, :].unsqueeze(1).broadcast_to([P, 2, EXPERTS]),
                                        tab[:, :, :], ALU.mult).then_inc(sel_chain.sem, 1)

            def expert_select(t):
                after(dve, sel_chain, t)
                nc.vector.tensor_reduce(sel[:, parity(t), :], sel_t[:, :, :], axis=AX.X, op=ALU.add) \
                    .then_inc(sel_done.sem, 1)

            def by_expert(t, c, to, src, src_done, done, free):
                if c == 0:
                    after(dve, maskT_done, t)
                    after(dve, src_done, t)
                    after(dve, free, shift(t, -1))
                nc.vector.tensor_tensor(to[:, c, :, :], maskT[:, parity(t), :, :],
                                        src[:, c, :].unsqueeze(1).broadcast_to([P, EXPERTS, P]),
                                        ALU.mult).then_inc(done.sem, 1)

            def hidden(t):
                after(dve, square_done, t)
                after(dve, h_m_done, shift(t, -1))
                nc.vector.tensor_tensor(h[:, :], g_square[:, :], gate_bank(t)[:, D:2 * D], ALU.mult) \
                    .then_inc(h_done.sem, 1)

            def hidden_max(t):
                after(dve, h_done, t)
                nc.vector.tensor_reduce(h_max[:, :], h[:, :], axis=AX.X, op=ALU.max, apply_absolute_value=True) \
                    .then_inc(h_chain.sem, 1)

            def hidden_abs(t):
                after(dve, h_chain, t, 1)
                after(dve, h_scale_done, t)
                after(dve, y_scale_done, shift(t, -1))
                nc.vector.tensor_scalar(h_abs[:, :], h_max[:, :], h_scale[:, parity(t), :], Q_EPS,
                                        ALU.mult, ALU.max).then_inc(h_chain.sem, 1)

            def hidden_inverse(t):
                after(dve, h_chain, t, 2)
                nc.vector.reciprocal(h_inv[:, :], h_abs[:, :]).then_inc(h_chain.sem, 1)

            def hidden_factor(t):
                after(dve, h_chain, t, 3)
                nc.vector.tensor_scalar(h_mul[:, :], h_inv[:, :], h_scale[:, parity(t), :], 127.0,
                                        ALU.mult, ALU.mult).then_inc(h_chain.sem, 1)

            def result(t):
                after(dve, y_psum, t)
                after(dve, y_scale_done, t)
                arrived(dve, y_out, t)
                p = parity(t)
                nc.vector.scalar_tensor_tensor(out=y[:, p, :], in0=ffn[:, 0:D], scalar=y_scale[:, :],
                                               in1=x2[:, x2_slot(t), :], op0=ALU.mult, op1=ALU.add) \
                    .then_inc(y_done.sem, 1)

            def tile_work(t):
                ahead, ahead2 = shift(t, 1), shift(t, 2)
                back1, ffn1, ffn2 = shift(t, -1), shift(t, -2), shift(t, -3)
                for u in range(PAIRS):
                    maxima(t, u + 2)
                    if number(t) == 0 and u + 1 < len(ABS_COUNTS):
                        first = 3 * ABS_SPLIT + sum(ABS_COUNTS[:u + 1])
                        for n in range(first, first + ABS_COUNTS[u + 1]):
                            weights_abs(n)
                    if u == 0:
                        if exists(ffn2):
                            hidden_inverse(ffn2)
                        if exists(ffn1):
                            expert_steps(ffn1)
                        if exists(ffn2):
                            hidden_factor(ffn2)
                        if exists(ffn1):
                            expert_select(ffn1)
                    if u == 1:
                        if exists(ffn1):
                            by_expert(ffn1, 0, am, aT, aT_done, am_done, gu_psum)
                        if exists(back1):
                            sums_inverse(back1)
                        if exists(ahead):
                            query_steps(ahead)
                        if exists(back1):
                            heads_normalised(back1)
                    if u == 2:
                        if exists(ffn2):
                            by_expert(ffn2, 0, hm, hT, hT_done, hm_done, y_psum)
                        if exists(ahead):
                            query_inverse(ahead)
                            query_scaled(ahead)
                            query_rounded(ahead)
                    if u == 3:
                        if exists(ahead2):
                            first_stats(ahead2)
                        if exists(ffn2):
                            by_expert(ffn2, 1, hm, hT, hT_done, hm_done, y_psum)
                        if exists(ahead):
                            query_copies(ahead)
                    if u == 4:
                        if exists(ffn2):
                            result(ffn2)
                        if exists(back1):
                            residual(back1)
                        if exists(ahead2):
                            first_aggregate(ahead2)
                        if exists(back1):
                            second_stats(back1)
                        if exists(ffn1):
                            by_expert(ffn1, 1, am, aT, aT_done, am_done, gu_psum)
                        if exists(back1):
                            second_aggregate(back1)
                    if u == 5:
                        if exists(back1):
                            second_norm(back1)
                        if exists(ahead2):
                            first_norm(ahead2)
                    if u == 6:
                        if exists(back1):
                            input_max(back1)
                            input_step(back1)
                            input_inverse(back1)
                    if u == 7:
                        if exists(back1):
                            logit_max(back1)
                        if exists(ffn1):
                            hidden(ffn1)
                        if exists(back1):
                            logit_rank(back1)
                        if exists(ffn1):
                            hidden_max(ffn1)
                        if exists(back1):
                            logit_top(back1)
                            expert_mask(back1)
                        if exists(ffn1):
                            hidden_abs(ffn1)
                    if number(t) == 0 and u == WP_AT:
                        output_rows()
                    if t[0] is None and 8 * t[1] + u == W_FROM - 1:
                        weight_steps()
                    if t[0] is None and 0 <= 8 * t[1] + u - W_FROM - 1 < 3 * EXPERTS // W_EACH:
                        weights_ternary(W_EACH * (8 * t[1] + u - W_FROM - 1))

            run(dve, tile_work)
            hidden_inverse(THIRD_LAST)
            sums_inverse(LAST)
            hidden_factor(THIRD_LAST)
            heads_normalised(LAST)
            expert_steps(NEXT_LAST)
            expert_select(NEXT_LAST)
            by_expert(NEXT_LAST, 0, am, aT, aT_done, am_done, gu_psum)
            by_expert(THIRD_LAST, 0, hm, hT, hT_done, hm_done, y_psum)
            residual(LAST)
            second_stats(LAST)
            second_aggregate(LAST)
            by_expert(THIRD_LAST, 1, hm, hT, hT_done, hm_done, y_psum)
            second_norm(LAST)
            input_max(LAST)
            input_step(LAST)
            input_inverse(LAST)
            by_expert(NEXT_LAST, 1, am, aT, aT_done, am_done, gu_psum)
            result(THIRD_LAST)
            logit_max(LAST)
            logit_rank(LAST)
            logit_top(LAST)
            expert_mask(LAST)
            expert_steps(LAST)
            expert_select(LAST)
            hidden(NEXT_LAST)
            hidden_max(NEXT_LAST)
            hidden_abs(NEXT_LAST)
            by_expert(LAST, 0, am, aT, aT_done, am_done, gu_psum)
            hidden_inverse(NEXT_LAST)
            hidden_factor(NEXT_LAST)
            by_expert(LAST, 1, am, aT, aT_done, am_done, gu_psum)
            for c in range(DC):
                by_expert(NEXT_LAST, c, hm, hT, hT_done, hm_done, y_psum)
            hidden(LAST)
            hidden_max(LAST)
            hidden_abs(LAST)
            hidden_inverse(LAST)
            hidden_factor(LAST)
            result(NEXT_LAST)
            for c in range(DC):
                by_expert(LAST, c, hm, hT, hT_done, hm_done, y_psum)
            result(LAST)

        @block.tensor
        def _(pe):
            def add_bias(to, which):
                nc.tensor.matmul(to, ones_b[:, 0:P], bias3[:, which * D:(which + 1) * D], start=True, stop=False)

            def product(to, lhs, rhs, biased=False):
                for c in range(DC):
                    last = nc.tensor.matmul(to, lhs(c), rhs(c), start=(c == 0 and not biased), stop=(c == DC - 1))
                return last

            def turn_norm(t, bank, ln, done, psum):
                after(pe, done, t)
                for c in range(DC):
                    last = nc.tensor.transpose(bank[:, c * P:(c + 1) * P], ln[:, c * P:(c + 1) * P], ident[:, :])
                last.then_inc(psum.sem, 1)

            def queries(t, c):
                if c == 0:
                    after(pe, lnT1_done, t)
                    add_bias(front[:, 0:D], 2)
                ins = nc.tensor.matmul(front[:, 0:D], lnT1[:, c, :], wq_sb[:, c, :], start=False, stop=(c == DC - 1))
                if c == DC - 1:
                    ins.then_inc(q_psum.sem, 1)

            def turn_queries(t):
                after(pe, q_rep_done, t)
                for p in range(PAIRS):
                    last = nc.tensor.transpose(front_b[:, p, :],
                                               q_rep[:, 2 * p:2 * p + 2, :, :].rearrange("p h r d -> p (h r d)"),
                                               ident_b[:, :])
                last.then_inc(qT_psum.sem, 1)

            def score(t, pair):
                t, pair = unit(t, pair)
                if not exists(t):
                    return
                if pair == 0:
                    after(pe, qT_done, t)
                before, b_pair = unit(t, pair - 2)
                for j in range(2):
                    after(pe, exp_done, before, 2 * b_pair + j + 1)
                    r = slice(j * SLOT, j * SLOT + ROWS)
                    last = nc.tensor.matmul(scores[pair % 2][:, j, :], qT[r, parity(t), pair, :],
                                            kT[r, pair, :], start=True, stop=True)
                last.then_inc(scores_done.sem, 1)

            def values(t, pair):
                t, pair = unit(t, pair)
                if not exists(t):
                    return
                if pair == 0:
                    if number(t) == 0:
                        pe.wait_ge(V_ready, 16 * DC)
                    after(pe, attn_done, shift(t, -1))
                    for k in range(KC):
                        nc.tensor.matmul(heads_out[:, 0:D], minus_off[:, :], V[:, k, :], start=(k == 0), stop=False)
                after(pe, probsT_done[pair % RING], t, 16 * (pair // RING + 1))
                for j in range(2):
                    hd = 2 * pair + j
                    for k in range(KC):
                        last = nc.tensor.matmul(heads_out[:, hd * HD:(hd + 1) * HD],
                                                probsT[:, pair % RING, j * KC + k, :],
                                                V[:, k, hd * HD:(hd + 1) * HD], start=False,
                                                stop=(hd == HEADS - 1 and k == KC - 1))
                last.then_inc(pv_done.sem, 1)

            pe.wait_ge(ones_ready, 1)
            pe.wait_ge(kv_bias_ready, 3)
            pe.wait_ge(got_kv, 32)
            for k in range(KC):
                add_bias(k_psum_v[:, k, :], 0)
                product(k_psum_v[:, k, :], lambda c: ctxT[:, c, k * P:(k + 1) * P], lambda c: wkv_sb[:, c, 0:D],
                        biased=True).then_inc(k_psum, 1)
                if k == 1:
                    pe.wait_ge(idents_ready, 2)
                    turn_norm((None, 0), front, ln1, ln1_done, lnT1_psum)
            for c in range(DC):
                nc.tensor.matmul(scores[1][:, c, :], bias3[:, D + c * P:D + (c + 1) * P], ones_b[:, :],
                                 start=True, stop=False)
                product(scores[1][:, c, :], lambda i: wkv_sb[:, i, D + c * P:D + (c + 1) * P],
                        lambda i: ctxT[:, i, :], biased=True).then_inc(v_psum, 1)
            pe.wait_ge(got_wq, 16)
            pe.wait_ge(qp_bias_ready, 3)
            for c in range(DC):
                queries((None, 0), c)
            for k in range(KC):
                pe.wait_ge(k_rep_ready, k // 2 + 1)
                if k == 3:
                    pe.wait_ge(kT_ready, 1)
                for p in range(PAIRS):
                    last = nc.tensor.transpose(key_banks[k][:, p, :],
                                               k_rep[:, k, 2 * p:2 * p + 2, :].rearrange("p h s -> p (h s)"),
                                               ident_b[:, :])
                last.then_inc(kT_psum, 1)
            turn_queries((None, 0))
            for i in range(2):
                pe.wait_ge(k_chain[i], 4)
            pe.wait_ge(kT_ready, KC)
            score((None, 0), 0)
            pe.wait_ge(v_chain, 2 * DC + 2)
            score((None, 0), 1)
            pe.wait_ge(qT_done.sem, 1)
            turn_norm((None, 1), front, ln1, ln1_done, lnT1_psum)

            FFN_PARTS = 4

            def gate_up(t, part):
                if part == 0:
                    if number(t) == 0:
                        pe.wait_ge(w_ready, 3 * EXPERTS // 2)
                        pe.wait_ge(w_ready_act, 3 * EXPERTS // 2)
                    if number(t) not in (TILES - 2, TILES - 1):
                        after(pe, y_done, shift(t, -1))
                each = DC * EXPERTS // FFN_PARTS
                if part * each % EXPERTS == 0:
                    after(pe, am_done, t, part * each // EXPERTS + 1)
                for i in range(part * each, (part + 1) * each):
                    c, e = i // EXPERTS, i % EXPERTS
                    last = nc.tensor.matmul(gate_bank(t), am[:, c, e, :],
                                            gu_w[:, c, e, :, :].rearrange("p a n -> p (a n)"),
                                            start=(i == 0), stop=(i == DC * EXPERTS - 1))
                if part == FFN_PARTS - 1:
                    last.then_inc(gu_psum.sem, 1)

            def projection(t):
                after(pe, attnT_done, t)
                if number(t) == 0:
                    pe.wait_ge(wp_ready, DC)
                add_bias(back[:, 0:D], 3)
                product(back[:, 0:D], lambda c: attnT[:, c, :], lambda c: wp_sb[:, c, :], biased=True) \
                    .then_inc(proj_psum.sem, 1)

            def route(t):
                if number(t) == 0:
                    pe.wait_ge(got_router, 16)
                after(pe, lnT2_done, t)
                product(back[:, 0:EXPERTS], lambda c: lnT2[:, c, :], lambda c: rT[:, c, :]) \
                    .then_inc(logits_psum.sem, 1)

            def spread_mask(t):
                after(pe, mask_done, t)
                for e in range(EXPERTS):
                    last = nc.tensor.transpose(mask_bank(t)[:, e, :], mask[:, e:e + 1].broadcast_to([P, P]),
                                               ident_b[:, :])
                last.then_inc(maskT_psum.sem, 1)

            def down(t, part):
                if part == 0:
                    if number(t) in (TILES - 2, TILES - 1):
                        after(pe, y_done, shift(t, -1))
                    else:
                        after(pe, h_done, t)
                each = DC * EXPERTS // FFN_PARTS
                if part * each % EXPERTS == 0:
                    after(pe, hm_done, t, part * each // EXPERTS + 1)
                for i in range(part * each, (part + 1) * each):
                    c, e = i // EXPERTS, i % EXPERTS
                    last = nc.tensor.matmul(ffn[:, 0:D], hm[:, c, e, :], dn_w[:, c, e, :],
                                            start=(i == 0), stop=(i == DC * EXPERTS - 1))
                if part == FFN_PARTS - 1:
                    last.then_inc(y_psum.sem, 1)

            def turn_attention(t):
                if number(t) != TILES - 1:
                    after(pe, maskT_done, shift(t, -1))
                turn_norm(t, back, attn, attn_done, attnT_psum)

            def turn_first_norm(t):
                after(pe, qT_done, shift(t, -1))
                turn_norm(t, front, ln1, ln1_done, lnT1_psum)

            def turn_second_norm(t):
                turn_norm(t, back, ln2, ln2_done, lnT2_psum)

            def tile_work(t):
                ahead, ahead2 = shift(t, 1), shift(t, 2)
                back1, ffn1, ffn2 = shift(t, -1), shift(t, -2), shift(t, -3)
                for u in range(PAIRS):
                    score(t, u + 2)
                    if u == 0:
                        if exists(ahead):
                            queries(ahead, 0)
                    if u == 4:
                        if exists(ffn2):
                            down(ffn2, 2)
                            down(ffn2, 3)
                    if u == 5:
                        if exists(ffn1):
                            gate_up(ffn1, 0)
                            gate_up(ffn1, 1)
                    if u == 6:
                        if exists(ffn1):
                            gate_up(ffn1, 2)
                            gate_up(ffn1, 3)
                    if u == 7:
                        if exists(back1):
                            turn_second_norm(back1)
                    values(t, u - LAG)
                    if u == 0:
                        if exists(ffn1):
                            spread_mask(ffn1)
                    if u == 1:
                        if exists(ahead):
                            queries(ahead, 1)
                    if u == 2:
                        if exists(back1):
                            turn_attention(back1)
                    if u == 3:
                        if exists(ffn2):
                            down(ffn2, 0)
                            down(ffn2, 1)
                        if exists(back1):
                            projection(back1)
                    if u == 4:
                        if exists(ahead):
                            turn_queries(ahead)
                    if u == 7:
                        if exists(ahead2):
                            turn_first_norm(ahead2)
                        if exists(back1):
                            route(back1)
                    if number(t) == 0 and u == W_FROM - 1:
                        pe.wait_ge(w_abs_ready, 3 * ABS_SPLIT)
                        pe.wait_ge(w_abs_ready_dve, 3 * (EXPERTS - ABS_SPLIT))
                        nc.tensor.matmul(ffn[:, 0:3 * EXPERTS], ones[:, :],
                                         w_abs[:, :, :].rearrange("p m e -> p (m e)"),
                                         start=True, stop=True).then_inc(w_sum_psum, 1)

            run(pe, tile_work)
            values(LAST, PAIRS - 2)
            values(LAST, PAIRS - 1)
            after(pe, mask_done, NEXT_LAST)
            turn_attention(LAST)
            spread_mask(NEXT_LAST)
            projection(LAST)
            for part in range(FFN_PARTS):
                down(THIRD_LAST, part)
            turn_second_norm(LAST)
            gate_up(NEXT_LAST, 0)
            gate_up(NEXT_LAST, 1)
            gate_up(NEXT_LAST, 2)
            route(LAST)
            gate_up(NEXT_LAST, 3)
            spread_mask(LAST)
            for part in range(FFN_PARTS):
                gate_up(LAST, part)
            for part in range(FFN_PARTS):
                down(NEXT_LAST, part)
            after(pe, h_q_done, LAST)
            for c in range(DC):
                last = nc.tensor.transpose(front_b[:, c, :], h_q[:, c * P:(c + 1) * P], ident_b[:, :])
            last.then_inc(last_hT_psum, 1)
            for part in range(FFN_PARTS):
                down(LAST, part)


def kernel(**inputs):
    import numpy as np
    import concourse.bacc as bacc
    from concourse.bass_utils import run_bass_kernel_spmd

    a = {k: np.asarray(v) for k, v in inputs.items()}
    batch, tokens, dim = a["x"].shape
    experts = a["L0_ffn_router_w"].shape[0]
    chunks = dim // 128

    def by_chunk(w):
        return w.transpose(2, 0, 1).reshape(chunks, 128, experts, -1)

    laid = {
        "x": a["x"].reshape(batch * tokens, dim),
        "ctx_t": a["ctx_2048"].reshape(-1, dim).T,
        "wq": a["L0_xattn_Wq"],
        "wkv": a["L0_xattn_Wkv"],
        "wp": a["L0_xattn_Wp"],
        "biases": np.concatenate([a["L0_xattn_bkv"], a["L0_xattn_bq"], a["L0_xattn_bp"]]).reshape(1, 4 * dim),
        "router": a["L0_ffn_router_w"].T.reshape(chunks, 128, experts),
        "w_experts": np.stack([by_chunk(a["L0_ffn_" + m]) for m in ("wg", "wu", "wd")], axis=3),
    }
    nc = bacc.Bacc("TRN2", target_bir_lowering=False, num_devices=1)
    arrays, args = {}, []
    for name, v in laid.items():
        v = np.ascontiguousarray(v)
        arrays[f"in_{name}"] = v
        args.append(nc.dram_tensor(f"in_{name}", v.shape, mybir.dt.from_np(v.dtype), kind="ExternalInput").ap())
    out = nc.dram_tensor("out_x", (batch * tokens, dim), mybir.dt.float32, kind="ExternalOutput").ap()
    cross_attention_moe(nc, *args, out)
    r = run_bass_kernel_spmd(nc, [arrays], core_ids=[0])
    return r.results[0]["out_x"].reshape(batch, tokens, dim)
```
